# Optimizing a Trainium2 kernel written in Bass

```python
import numpy as np
import jax
import jax.numpy as jnp

def _softmax(x, axis=-1):
    return jax.nn.softmax(x, axis=axis)

def _gelu(x):
    return jax.nn.gelu(x, approximate=True)

def _silu(x):
    return jax.nn.silu(x)

def _sigmoid(x):
    return jax.nn.sigmoid(x)

def _layernorm(x, axis=-1, eps=1e-05):
    m = jnp.mean(x, axis=axis, keepdims=True)
    v = jnp.var(x, axis=axis, keepdims=True)
    return (x - m) / jnp.sqrt(v + eps)

def _scatter_add(tgt, idx, src, axis=0):
    return tgt.at[idx].add(src)

def _segment_sum(src, seg, n):
    return jax.ops.segment_sum(src, seg, n)
kernel_name = 'mk_flamingo_gated_d1_seqx_r8_297648'

def setup_inputs(seed: int=0):
    np.random.seed(seed)
    _w = jnp.asarray

    def _rec_inputs():
        import jax
        import jax.numpy as jnp
        _rk = jax.random.key(seed)
        x = -0.0002928 + 1 * jax.random.normal(jax.random.fold_in(_rk, 1), (1, 1024, 128), jnp.float32)
        _lenS = 1024 - jax.random.randint(jax.random.fold_in(_rk, 7), (1,), 0, max(1, 1024 // 4) + 1, jnp.int32)
        _lenS2 = 6404 - jax.random.randint(jax.random.fold_in(_rk, 8), (1,), 0, max(1, 6404 // 4) + 1, jnp.int32)
        _ctx_2048P = jax.random.normal(jax.random.fold_in(_rk, 11), (1, 16, 256), jnp.float32)
        _ctx_2048c = jax.random.dirichlet(jax.random.fold_in(_rk, 511), 0.3 * jnp.ones((16,), jnp.float32), (1, 6404))
        _ctx_2048t = jnp.einsum('bsk,bkd->bsd', _ctx_2048c, _ctx_2048P)
        _ctx_2048t = _ctx_2048t * jax.lax.rsqrt(jnp.mean(jnp.square(_ctx_2048t)) + 1e-12) * 0.953939
        ctx_2048 = -0.000514642 + 1.00011 * (_ctx_2048t + 0.3 * jax.random.normal(jax.random.fold_in(_rk, 611), (1, 6404, 256), jnp.float32))
        _g = jax.random.normal(jax.random.fold_in(_rk, 9001), (2, 1), jnp.float32)
        _g = jnp.sign(_g) * jnp.maximum(jnp.abs(_g), 1.0) + (_g == 0) * 1.0
        g_xattn = _g[0]
        g_ffn = _g[1]
        return (x, ctx_2048, g_xattn, g_ffn)
    x, ctx_2048, g_xattn, g_ffn = _rec_inputs()

    def _L0_xattn_setup():
        import jax, jax.numpy as jnp
        import numpy as np
        NUM_HEADS = 16
        key = jax.random.key(seed)
        ks = jax.random.split(key, 5)
        dim = 128
        B, N, N_c = (4, 128, 32)
        x = jax.random.normal(ks[0], (B, N, dim), dtype=jnp.float32)
        context = jax.random.normal(ks[1], (B, N_c, 2 * dim), dtype=jnp.float32)
        w_qkv = jax.random.normal(ks[2], (3 * dim, dim), dtype=jnp.float32) * 0.02
        w_proj = jax.random.normal(ks[3], (dim, dim), dtype=jnp.float32) * 0.02
        b_proj = jax.random.normal(ks[4], (dim,), dtype=jnp.float32) * 0.02
        return {'x': x, 'context': context, 'w_qkv': w_qkv, 'w_proj': w_proj, 'b_proj': b_proj}
    _L0_xattn_all = _L0_xattn_setup()
    _L0_xattn_in = {k: v for k, v in _L0_xattn_all.items() if k in ('w_qkv', 'w_proj', 'b_proj')}
    del _L0_xattn_all

    def _L0_ffn_setup():
        import jax, jax.numpy as jnp
        import numpy as np
        NUM_EXPERTS = 8
        N_EMBD = 128
        D_FF = 4 * N_EMBD
        B, S = (4, 256)
        key = jax.random.key(seed)
        ks = jax.random.split(key, 6)
        x = jax.random.normal(ks[0], (B, S, N_EMBD), dtype=jnp.float32)
        gate_w = jax.random.normal(ks[1], (N_EMBD, NUM_EXPERTS), dtype=jnp.float32) * 0.02
        w1 = jax.random.normal(ks[2], (NUM_EXPERTS, N_EMBD, D_FF), dtype=jnp.float32) * 0.02
        b1 = jnp.zeros((NUM_EXPERTS, D_FF), dtype=jnp.float32)
        w2 = jax.random.normal(ks[3], (NUM_EXPERTS, D_FF, N_EMBD), dtype=jnp.float32) * 0.02
        b2 = jnp.zeros((NUM_EXPERTS, N_EMBD), dtype=jnp.float32)
        return {'x': x, 'gate_w': gate_w, 'w1': w1, 'b1': b1, 'w2': w2, 'b2': b2}
    _L0_ffn_all = _L0_ffn_setup()
    _L0_ffn_in = {k: v for k, v in _L0_ffn_all.items() if k in ('gate_w', 'w1', 'b1', 'w2', 'b2')}
    del _L0_ffn_all
    return {'x': x, 'ctx_2048': ctx_2048, 'g_xattn': g_xattn, 'g_ffn': g_ffn, 'L0_xattn_w_qkv': _L0_xattn_in['w_qkv'], 'L0_xattn_w_proj': _L0_xattn_in['w_proj'], 'L0_xattn_b_proj': _L0_xattn_in['b_proj'], 'L0_ffn_gate_w': _L0_ffn_in['gate_w'], 'L0_ffn_w1': _L0_ffn_in['w1'], 'L0_ffn_b1': _L0_ffn_in['b1'], 'L0_ffn_w2': _L0_ffn_in['w2'], 'L0_ffn_b2': _L0_ffn_in['b2']}

def reference(x, ctx_2048, g_xattn, g_ffn, L0_xattn_w_qkv, L0_xattn_w_proj, L0_xattn_b_proj, L0_ffn_gate_w, L0_ffn_w1, L0_ffn_b1, L0_ffn_w2, L0_ffn_b2):
    import jax
    import jax.numpy as jnp

    def _L0_xattn_ref(x, context, w_qkv, w_proj, b_proj):
        import jax, jax.numpy as jnp
        import numpy as np
        NUM_HEADS = 16
        B, N, C = x.shape
        H = NUM_HEADS
        D = C // H
        scale = D ** (-0.5)
        qkv = (x @ w_qkv.T).reshape(B, N, 3, H, D).transpose(2, 0, 3, 1, 4)
        q, k, v = (qkv[0], qkv[1], qkv[2])
        N_c = context.shape[1]
        kv = context.reshape(B, N_c, 2, H, D).transpose(2, 0, 3, 1, 4)
        extra_k, extra_v = (kv[0], kv[1])
        k = jnp.concatenate([extra_k, k], axis=2)
        v = jnp.concatenate([extra_v, v], axis=2)
        dtype = q.dtype
        attn = jnp.einsum('bhnd,bhmd->bhnm', q * scale, k).astype(jnp.float32)
        attn = jax.nn.softmax(attn, axis=-1).astype(dtype)
        out = jnp.einsum('bhnm,bhmd->bhnd', attn, v)
        out = out.transpose(0, 2, 1, 3).reshape(B, N, C)
        return out @ w_proj.T + b_proj

    def _L0_ffn_ref(x, gate_w, w1, b1, w2, b2):
        import jax, jax.numpy as jnp
        import numpy as np
        NUM_EXPERTS = 8
        N_EMBD = 128
        D_FF = 4 * N_EMBD
        B, S = (4, 256)
        Bb, Ss, D = x.shape
        x_flat = x.reshape(-1, D)
        router_logits = x_flat @ gate_w
        router_probs = jax.nn.softmax(router_logits, axis=-1)
        expert_idx = jnp.argmax(router_probs, axis=-1)
        expert_w = jnp.take_along_axis(router_probs, expert_idx[:, None], axis=1)[:, 0]
        out = jnp.zeros_like(x_flat)
        for e in range(NUM_EXPERTS):
            h = jax.nn.gelu(x_flat @ w1[e] + b1[e], approximate=False)
            y = h @ w2[e] + b2[e]
            sel = expert_idx == e
            out = out + jnp.where(sel, expert_w, 0.0)[:, None] * y
        return out.reshape(Bb, Ss, D)
    x = x + jnp.tanh(g_xattn[0]) * _L0_xattn_ref(_layernorm(x, axis=-1), ctx_2048, L0_xattn_w_qkv, L0_xattn_w_proj, L0_xattn_b_proj)
    x = x + jnp.tanh(g_ffn[0]) * _L0_ffn_ref(_layernorm(x, axis=-1), L0_ffn_gate_w, L0_ffn_w1, L0_ffn_b1, L0_ffn_w2, L0_ffn_b2)
    return x

_drawn_inputs = setup_inputs


def setup_inputs(seed=0):
    import zlib

    import numpy as np

    out = dict(_drawn_inputs(seed))
    spreads = {'L0_ffn_b1': (0.0, 0.8), 'L0_ffn_b2': (0.0, 0.498)}
    factors = {'L0_xattn_w_qkv': 8.0,
     'L0_xattn_b_proj': 3.617,
     'L0_ffn_gate_w': 3.248,
     'L0_ffn_w1': 6.518,
     'L0_ffn_w2': 5.905}
    for name, (base, spread) in spreads.items():
        noise = np.random.default_rng([zlib.crc32(name.encode()), seed]).standard_normal(out[name].shape)
        drawn = base * np.exp(spread * noise) if base else spread * noise
        out[name] = jnp.asarray(drawn.astype(out[name].dtype))
    for name, factor in factors.items():
        out[name] = (out[name] * factor).astype(out[name].dtype)
    return out
```

```python
from contextlib import ExitStack

import concourse.bass as bass
from concourse import mybir

F32 = mybir.dt.float32
BF16 = mybir.dt.bfloat16
I32 = mybir.dt.int32
ALU = mybir.AluOpType
ACT = mybir.ActivationFunctionType
AX = mybir.AxisListType

P = 128
BANK = 512

TOKENS, C = 1024, 128
CTX = 6404
HEADS, D = 16, 8
EXPERTS, FF = 8, 512
FFC = FF // P
TT = TOKENS // P
HALF = BANK
GROUPS = 4
GH = HEADS // GROUPS
PAIRS = HEADS // 2

CT = CTX // P
REST = CTX - CT * P
NT = TT + CT + 1
KEYS = NT * P
STAGE = 10

Q_PART = (0, 0, 1, 1, 0, 2)
K_PART = (0, 1, 0, 1, 2, 0)
SLOTS = len(Q_PART)
SHIFT = SLOTS * D
ROWS = SHIFT + 3

CHUNK = 3
CHUNKS = (NT + CHUNK - 1) // CHUNK
STEP = 2 * CHUNK
STEPS = NT // STEP
ACTS = 2 * NT
UNITS = 2 * GROUPS

SB, EB, PB, OB, GB, YB = 8, 3, 4, 2, 4, 8

WARM = 14

SCALE = float(D) ** -0.5
EPS = 1e-5
L_MIN = 2.0 ** -60
BOUND_SLACK = 1.0 + 2.0 ** -10
BOUND_MAX = 1.0e38


def program(nc, x, ctx_in, g_xattn, g_ffn, w_qkv, w_proj, b_proj, gate_w, w1, b1, w2, b2, out, kp, qp, mp, wpt):
    with ExitStack() as st:
        def sb(name, shape, dt=F32):
            return st.enter_context(nc.sbuf_tensor(name, shape, dt))

        def psum(name, shape, dt=F32):
            return st.enter_context(nc.psum_tensor(name, shape, dt))

        def sem(name):
            return st.enter_context(nc.semaphore(name))

        S = psum("S", [P, 6, BANK])
        O = psum("O", [P, 2, BANK])

        kst = sb("kst", [P, 4, KEYS], BF16)
        vres = sb("vres", [P, NT, HEADS, D + 1])
        qst = sb("qst", [P, PAIRS, TOKENS], BF16)
        work = sb("work", [P, CT * 2 * C])
        ctx_sb = work[:, :].rearrange("p (t c) -> p t c", c=2 * C)
        probs = work[:, 0:2 * 4 * BANK].rearrange("p (s h q) -> p s h q", s=2, h=4)
        U = work[:, 12 * BANK:12 * BANK + GROUPS * TOKENS].rearrange("p (g q) -> p g q", g=GROUPS)
        hT = work[:, 0:2 * FFC * BANK].rearrange("p (s f q) -> p s f q", s=2, f=FFC)
        w1_sb = work[:, 20 * BANK:20 * BANK + 2 * FF].rearrange("p (s f) -> p s f", s=2)
        w2_sb = work[:, 22 * BANK:22 * BANK + 2 * FFC * C].rearrange("p (s f c) -> p s f c", s=2, f=FFC)
        runmax = work[:, 0:4 * BANK].rearrange("p (h q) -> p h q", h=4)
        allmax = work[:, 4 * BANK:8 * BANK]
        mrow = work[0:1, 8 * BANK:12 * BANK]
        mrest = work[0:1, 4 * BANK:8 * BANK]
        rowparts = work[0:1, 12 * BANK:18 * BANK].bitcast(BF16).rearrange("p (i q) -> p i q", i=3)
        tail = sb("tail", [P, 2 * C])
        kring = sb("kring", [P, 2, 2, CHUNK * P], BF16)
        vring = sb("vring", [P, 2, CHUNK, GH, 32])
        qbuf = sb("qbuf", [P, 2, 2, HALF], BF16)
        xs = sb("xs", [P, TT, C])
        xn = sb("xn", [P, TT, C])
        xT = sb("xT", [P, TOKENS])
        qsc = xn[:, :, :].rearrange("p t c -> p (t c)")
        rest = sb("rest", [P, 2, BANK])
        parts = sb("parts", [P, 2, 3, BANK], BF16)
        mneg = rest[0:HEADS, :, :]
        mrem = qsc[0:HEADS, :].rearrange("p (s q) -> p s q", s=2)
        mparts = parts[0:HEADS, :, :, :]
        wq_sb = sb("wq_sb", [P, 3, C])
        wT = sb("wT", [P, 3 * C])
        wp_sb = sb("wp_sb", [P, C])
        wpT_sb = sb("wpT_sb", [P, C])
        wps = sb("wps", [P, GROUPS, C])
        ident = sb("ident", [P, P])
        blk = sb("blk", [P, HEADS])
        blk_k = sb("blk_k", [P, HEADS])
        selL = sb("selL", [P, P])
        ones1 = sb("ones1", [1, P])
        brow = sb("brow", [1, C])
        b2row = qst[0:1, 0:2, :].rearrange("p w q -> p (w q)").bitcast(F32).rearrange("p (e c) -> p e c", c=C)
        b1_sb = sb("b1_sb", [P, FFC, EXPERTS])
        b1_now = sb("b1_now", [P, 2, FFC])
        gw_sb = sb("gw_sb", [P, EXPERTS])
        gates = sb("gates", [P, 2])
        tg = sb("tg", [P, 2])
        stats = sb("stats", [P, TT, 6])
        mv = sb("mv", [P, TT, 2])
        std = sb("std", [P, TT])
        rstd = sb("rstd", [P, TT])
        kabs = sb("kabs", [P, 16])
        kmax = sb("kmax", [P, 1])
        lmin = sb("lmin", [P, UNITS])
        lneg = sb("lneg", [P, 1])
        lall = sb("lall", [P, 1])
        lflag = sb("lflag", [P, 1], I32)
        lg = sb("lg", [P, TT, EXPERTS])
        lt = sb("lt", [P, TT, EXPERTS])
        le = sb("le", [P, TT, EXPERTS])
        cand = sb("cand", [P, TT, EXPERTS])
        iota8 = sb("iota8", [P, TT, EXPERTS])
        rw = sb("rw", [P, TT, EXPERTS])
        r1 = sb("r1", [P, 4, TT])
        linv = rest

        x_in = sem("x_in")
        w_in = sem("w_in")
        small_in = sem("small_in")
        tail_in = sem("tail_in")
        pool_step = sem("pool_step")
        consts_done = sem("consts_done")
        wps_zero = sem("wps_zero")
        values_done = sem("values_done")
        ln_stats = sem("ln_stats")
        std_done = sem("std_done")
        xn_done = sem("xn_done")
        transposed = sem("transposed")
        evacuated = sem("evacuated")
        v_self = sem("v_self")
        v_self_out = sem("v_self_out")
        block_ready = sem("block_ready")
        part1_done = sem("part1_done")
        rest_done = sem("rest_done")
        block_read = sem("block_read")
        part2_done = sem("part2_done")
        part3_done = sem("part3_done")
        kmax_done = sem("kmax_done")
        qabs_done = sem("qabs_done")
        bound_done = sem("bound_done")
        bound_parts = sem("bound_parts")
        mp_out = sem("mp_out")
        q_stack_in = sem("q_stack_in")
        k_stack_in = sem("k_stack_in")
        wpt_ready = sem("wpt_ready")
        wpt_out = sem("wpt_out")
        wps_in = sem("wps_in")
        scores_ready = sem("scores_ready")
        exp_done = sem("exp_done")
        probs_used = sem("probs_used")
        k_ready = sem("k_ready")
        v_ready = sem("v_ready")
        q_ready = sem("q_ready")
        o_copied = sem("o_copied")
        attention_start = sem("attention_start")
        l_ready = sem("l_ready")
        linv_done = sem("linv_done")
        normed = sem("normed")
        dve_step = sem("dve_step")
        act_step = sem("act_step")
        lneg_done = sem("lneg_done")
        lall_done = sem("lall_done")
        flag_done = sem("flag_done")
        proj_done = sem("proj_done")
        x1_stats = sem("x1_stats")
        std2_done = sem("std2_done")
        x2n_done = sem("x2n_done")
        transposed2 = sem("transposed2")
        evacuated2 = sem("evacuated2")
        logits_ready = sem("logits_ready")
        shifted_logits = sem("shifted_logits")
        router_exp = sem("router_exp")
        gates_done = sem("gates_done")
        hidden_ready = sem("hidden_ready")
        gelu_done = sem("gelu_done")
        y_ready = sem("y_ready")
        y_added = sem("y_added")
        out_written = sem("out_written")
        fb_k = sem("fb_k")
        fb_s = sem("fb_s")
        fb_m = sem("fb_m")
        fb_max = sem("fb_max")
        fb_all = sem("fb_all")
        fb_rows = sem("fb_rows")
        fb_rows_in = sem("fb_rows_in")
        fb_units = sem("fb_units")
        fb_neg = sem("fb_neg")
        b2_in = sem("b2_in")
        bias_done = sem("bias_done")
        x1_done = sem("x1_done")
        tail_step = sem("tail_step")
        ctx_in_part = [sem(f"ctx_in_part{i}") for i in range(CT // STAGE)]
        parts_out = [sem("parts_out0"), sem("parts_out1")]
        expert_in = [sem("expert_in0"), sem("expert_in1")]

        block = st.enter_context(nc.Block())

        OWN = 4
        CBLOCKS = (CT + 1 + 3) // 4
        BLOCKS = OWN + CBLOCKS

        def block_tiles(b):
            return min(4, CT + 1 - 4 * b)

        def width(n):
            return BANK if n < OWN else block_tiles(n - OWN) * P

        def bank_of(n):
            return S[:, 2 + n, 0:width(n)] if n < OWN else S[:, (n - OWN) % 6, 0:width(n)]

        ctx_main = ctx_in[0, 0:CT * P, :].rearrange("(p t) c -> p t c", t=CT)
        LOADS = 2 * SLOTS

        def load_stack(sp, dst, first_pair, pairs, src, part, signal):
            for par in range(2):
                for slot in range(SLOTS):
                    rows = src[part[slot]].rearrange("(w a d) k -> a d w k", a=2, d=D)[par, :, first_pair:first_pair + pairs, :]
                    r = 64 * par + D * slot
                    sp.dma_start(dst[r:r + D, :, :], rows).then_inc(signal, 16)

        @block.sync
        def _(sp):
            sp.dma_start(xs[:, :, :], x.rearrange("a (p t) c -> p (a t) c", t=TT)).then_inc(x_in, 16)
            sp.dma_start(wq_sb[:, :, :], w_qkv.rearrange("(t p) c -> p t c", p=P)).then_inc(w_in, 16)
            sp.dma_start(wp_sb[:, :], w_proj).then_inc(w_in, 16)
            for i in range(CT // STAGE):
                sp.dma_start(ctx_sb[:, i * STAGE:(i + 1) * STAGE, :],
                             ctx_main[:, i * STAGE:(i + 1) * STAGE, :]).then_inc(ctx_in_part[i], 16)
            sp.dma_start(tail[0:REST, :], ctx_in[0, CT * P:CTX, :]).then_inc(tail_in, 16)
            sp.dma_start(tail[REST:P, :], ctx_in[0, CTX - 1:CTX, :].broadcast_to([P - REST, 2 * C])).then_inc(tail_in, 16)
            sp.dma_start(gates[:, 0:1], g_xattn.rearrange("(a b) -> a b", a=1).broadcast_to([P, 1])).then_inc(small_in, 16)
            sp.dma_start(gates[:, 1:2], g_ffn.rearrange("(a b) -> a b", a=1).broadcast_to([P, 1])).then_inc(small_in, 16)
            sp.dma_start(brow[:, :], b_proj.rearrange("(a c) -> a c", a=1)).then_inc(small_in, 16)
            with nc.allow_non_contiguous_dma(reason="16 KB of biases, once"):
                for f in range(FFC):
                    sp.dma_start(b1_sb[:, f, :], b1[:, f * P:(f + 1) * P].rearrange("e p -> p e")).then_inc(small_in, 16)
            sp.dma_start(gw_sb[:, :], gate_w).then_inc(small_in, 16)
            for n in range(BLOCKS):
                sp.wait_ge(part3_done, n + 1)
                w = width(n)
                dst = qp[:, :, n * BANK:n * BANK + w] if n < 2 else kp[:, :, (n - 2) * BANK:(n - 2) * BANK + w]
                sp.dma_start(dst.rearrange("i p k -> p i k"), parts[:, n % 2, :, 0:w]).then_inc(parts_out[n % 2], 16)
            sp.wait_ge(wpt_ready, 1)
            sp.dma_start(wpt, wpT_sb[:, :]).then_inc(wpt_out, 16)
            sp.wait_ge(parts_out[0], 16 * ((BLOCKS + 1) // 2))
            sp.wait_ge(parts_out[1], 16 * (BLOCKS // 2))
            sp.wait_ge(consts_done, 1)
            load_stack(sp, kst[:, 0:2, :], 0, 2, kp, K_PART, k_stack_in)
            load_stack(sp, qst[:, :, :], 0, PAIRS, qp, Q_PART, q_stack_in)
            sp.wait_ge(bound_parts, 1)
            sp.dma_start(mp.rearrange("i h k -> h i k"),
                         mparts.rearrange("h s i k -> h (s i k)").rearrange("h (i k) -> h i k", i=3)).then_inc(mp_out, 16)
            sp.wait_ge(mp_out, 16)
            for par in range(2):
                rows = mp.rearrange("i (w a) k -> a i w k", a=2)[par]
                sp.dma_start(qst[64 * par + SHIFT:64 * par + ROWS, :, :], rows).then_inc(q_stack_in, 16)
            sp.wait_ge(wpt_out, 16)
            sp.wait_ge(wps_zero, 1)
            for j in range(GH):
                sp.dma_start(wps[32 * j:32 * j + D, :, :],
                             wpt.rearrange("(g j d) c -> j d g c", j=GH, d=D)[j]).then_inc(wps_in, 16)
            sp.wait_ge(values_done, 1 + CT // STAGE + 1)
            sp.wait_ge(block_read, BLOCKS)
            for e in range(2):
                sp.dma_start(w1_sb[:, e, :], w1[e]).then_inc(expert_in[e], 16)
                sp.dma_start(w2_sb[:, e, :, :], w2[e].rearrange("(f p) c -> p f c", p=P)).then_inc(expert_in[e], 16)

            def load_group(number, group):
                sp.wait_ge(k_stack_in, 16 * LOADS * number)
                b = 2 * (group % 2)
                load_stack(sp, kst[:, b:b + 2, :], 2 * group, 2, kp, K_PART, k_stack_in)

            for g in range(1, GROUPS):
                if g >= 2:
                    sp.wait_ge(o_copied, OB + 2 * (g - 1))
                load_group(g, g)

            sp.wait_ge(flag_done, 1)
            redo = sp.value_load(lflag[0:1, 0:1], min_val=0, max_val=1)
            with sp.If(redo > 0):
                for g in range(GROUPS):
                    if g >= 2:
                        sp.wait_ge(fb_units, 2 * (g - 1))
                    load_group(GROUPS + g, g)
                    for half in range(2):
                        sp.wait_ge(fb_rows, 2 * g + half + 1)
                        for par in range(2):
                            for i in range(3):
                                r = 64 * par + SHIFT + i
                                heads = rowparts[:, i, :].rearrange("p (w a q) -> p a w q", w=2, a=2)[:, par, :, :]
                                sp.dma_start(qst[r:r + 1, 2 * g:2 * g + 2, half * HALF:(half + 1) * HALF],
                                             heads).then_inc(fb_rows_in, 16)
                for g in range(GROUPS):
                    if g < 2:
                        sp.wait_ge(fb_units, 2 * (g + 3))
                    else:
                        sp.wait_ge(o_copied, OB + UNITS + 2 * (g - 1))
                    load_group(2 * GROUPS + g, g)
                sp.wait_ge(normed, 2)

            sp.wait_ge(normed, 1)
            sp.dma_start(b2row, b2.rearrange("(a e) c -> a e c", a=1)).then_inc(b2_in, 16)
            for e in range(2, EXPERTS):
                sp.wait_ge(y_ready, YB + 8 * (e - 1))
                sp.wait_ge(expert_in[e % 2], 32 * (e // 2))
                sp.dma_start(w1_sb[:, e % 2, :], w1[e]).then_inc(expert_in[e % 2], 16)
                sp.dma_start(w2_sb[:, e % 2, :, :], w2[e].rearrange("(f p) c -> p f c", p=P)).then_inc(expert_in[e % 2], 16)
            sp.wait_ge(y_added, YB + 8 * EXPERTS)
            sp.dma_start(out.rearrange("a (p t) c -> p (a t) c", t=TT), xs[:, :, :]).then_inc(out_written, 16)
            sp.wait_ge(out_written, 16)

        @block.gpsimd
        def _(pool):
            nc.gpsimd.memset(ident[:, :], 0.0).then_inc(pool_step, 1)
            nc.gpsimd.memset(blk[:, :], 1.0).then_inc(pool_step, 1)
            nc.gpsimd.memset(selL[:, :], 0.0).then_inc(pool_step, 1)
            pool.wait_ge(pool_step, 3)
            nc.gpsimd.affine_select(out=ident[:, :], in_=ident[:, :], compare_op=ALU.not_equal, fill=1.0,
                                    base=0, pattern=[[-1, P]], channel_multiplier=1).then_inc(pool_step, 1)
            nc.gpsimd.affine_select(out=blk[:, :], in_=blk[:, :], compare_op=ALU.is_ge, fill=0.0,
                                    base=0, pattern=[[-D, HEADS]], channel_multiplier=1).then_inc(pool_step, 1)
            pool.wait_ge(pool_step, 5)
            nc.gpsimd.affine_select(out=blk[:, :], in_=blk[:, :], compare_op=ALU.is_ge, fill=0.0,
                                    base=D - 1, pattern=[[D, HEADS]], channel_multiplier=-1).then_inc(pool_step, 1)
            sel4 = selL[:, :].rearrange("p (j r) -> p j r", j=GH)
            nc.gpsimd.affine_select(out=sel4, in_=sel4, compare_op=ALU.not_equal, fill=1.0,
                                    base=-D, pattern=[[-32, GH], [0, 32]], channel_multiplier=1).then_inc(pool_step, 1)
            nc.gpsimd.iota(iota8[:, :, :], pattern=[[0, TT], [1, EXPERTS]], base=0, channel_multiplier=0,
                           allow_small_or_imprecise_dtypes=True).then_inc(pool_step, 1)
            for par in range(2):
                r = slice(64 * par + 32, 64 * par + 64)
                pool.wait_ge(pool_step, 8 + 2 * par)
                nc.gpsimd.memset(kst[r, :, :], 1.0).then_inc(pool_step, 1)
                pool.wait_ge(pool_step, 9 + 2 * par)
                nc.gpsimd.memset(qst[r, :, :], 0.0).then_inc(pool_step, 1)
            pool.wait_ge(pool_step, 12)
            nc.gpsimd.memset(wps[:, :, :], 0.0).then_inc(wps_zero, 1)
            nc.gpsimd.memset(ones1[:, :], 1.0).then_inc(consts_done, 1)
            nc.gpsimd.memset(vring[:, :, :, :, :], 0.0).then_inc(pool_step, 1)
            nc.gpsimd.memset(vres[:, 0:NT - 1, :, D:D + 1], 1.0).then_inc(pool_step, 1)
            nc.gpsimd.memset(vres[:, NT - 1, :, :], 0.0).then_inc(pool_step, 1)
            pool.wait_ge(pool_step, 15)
            nc.gpsimd.memset(vres[0:REST, NT - 1, :, D:D + 1], 1.0).then_inc(values_done, 1)
            for i in range(CT // STAGE):
                pool.wait_ge(ctx_in_part[i], 16)
                src = ctx_sb[:, i * STAGE:(i + 1) * STAGE, C:2 * C].rearrange("p t (h d) -> p t h d", d=D)
                nc.gpsimd.tensor_copy(vres[:, TT + i * STAGE:TT + (i + 1) * STAGE, :, 0:D], src).then_inc(values_done, 1)
            pool.wait_ge(tail_in, 32)
            nc.gpsimd.tensor_copy(vres[0:REST, NT - 1, :, 0:D],
                                  tail[0:REST, C:2 * C].rearrange("p (h d) -> p h d", d=D)).then_inc(values_done, 1)
            pool.wait_ge(lneg_done, 1)
            nc.gpsimd.partition_all_reduce(lall[:, :], lneg[:, :], P, bass.bass_isa.ReduceOp.max).then_inc(lall_done, 1)
            pool.wait_ge(flag_done, 1)
            redo = pool.value_load(lflag[0:1, 0:1], min_val=0, max_val=1)
            with pool.If(redo > 0):
                for u in range(UNITS):
                    pool.wait_ge(fb_max, u + 1)
                    nc.gpsimd.partition_all_reduce(allmax, work[:, 0:4 * BANK], P,
                                                   bass.bass_isa.ReduceOp.max).then_inc(fb_all, 1)

        def attention_pe(pe, base):
            def scores(half, t, u, step=0):
                c = t // CHUNK
                early = int(half == 0 and t == 0)
                if t % CHUNK == 0:
                    pe.wait_ge(k_ready, u * CHUNKS + (c + 1) + step * 2)
                for a in range(2):
                    slot = (ACTS * half + 2 * t + a) % 3
                    pe.wait_ge(exp_done, u * ACTS + (2 * t + a - 2 + early + EB) + step * 2 * STEP)
                    for h in range(2):
                        r = slice(64 * h, 64 * h + ROWS)
                        k = kring[r, c % 2, a, (t % CHUNK) * P:(t % CHUNK + 1) * P]
                        last = nc.tensor.matmul(S[:, 2 * slot + h, :], k, qbuf[r, half, a, :], start=True, stop=True)
                    last.then_inc(scores_ready, 1)

            def values(half, t, u, step=0, start=False, stop=False):
                c = t // CHUNK
                if t % CHUNK == 0:
                    pe.wait_ge(v_ready, u * CHUNKS + (c + 1) + step * 2)
                pe.wait_ge(exp_done, u * ACTS + (2 * t + 2 + EB) + step * 2 * STEP)
                ps = (NT * half + t) % 2
                for j in range(GH):
                    last = nc.tensor.matmul(O[32 * j:32 * j + 32, half, :], vring[:, c % 2, t % CHUNK, j, :],
                                            probs[:, ps, j, :], start=start, stop=stop, tile_position=(0, 32 * j))
                last.then_inc(probs_used, 1)

            def group(g, last_group):
                for half in range(2):
                    u = g * 2 + (UNITS * base + half)
                    pe.wait_ge(o_copied, u + (OB - 1))
                    scores(half, 1, u)
                    values(half, 0, u, start=True)
                    for t in range(1, STEP):
                        scores(half, t + 1, u)
                        values(half, t, u)
                    with pe.Fori(1, STEPS) as i:
                        for t in range(STEP):
                            scores(half, t + 1, u, i)
                            values(half, t, u, i)
                    for t in range(STEPS * STEP, NT - 1):
                        scores(half, t + 1, u)
                        values(half, t, u)
                    if not (last_group and half == 1):
                        pe.wait_ge(q_ready, u + 2)
                        scores(1 - half, 0, u + 1)
                    values(half, NT - 1, u, stop=True)

            pe.wait_ge(q_ready, UNITS * base + 1)
            scores(0, 0, UNITS * base)
            with pe.Fori(0, GROUPS - 1) as g:
                group(g, False)
            group(GROUPS - 1, True)

        def spread_sums_pe(pe, base):
            for i in range(UNITS):
                pe.wait_ge(o_copied, OB + UNITS * base + i + 1)
                if i >= 2 or base:
                    pe.wait_ge(linv_done, UNITS * base + i - 1)
                nc.tensor.matmul(S[:, i % 2, :], selL[:, :], U[:, i // 2, (i % 2) * HALF:(i % 2 + 1) * HALF],
                                 start=True, stop=True).then_inc(l_ready, 1)

        @block.tensor
        def _(pe):
            pe.sem_inc(scores_ready, SB)
            pe.sem_inc(probs_used, PB)
            pe.sem_inc(y_ready, YB)
            pe.wait_ge(pool_step, 8)
            pe.wait_ge(w_in, 32)
            for i in range(3):
                nc.tensor.transpose(O[:, 0, i * P:(i + 1) * P], wq_sb[:, i, :], ident[:, :])
            nc.tensor.transpose(O[:, 0, 3 * P:4 * P], wp_sb[:, :], ident[:, :]).then_inc(transposed, 1)
            for t in range(TT):
                pe.wait_ge(xn_done, t + 1)
                last = nc.tensor.transpose(S[:, t // 4, (t % 4) * P:(t % 4 + 1) * P], xn[:, t, :], ident[:, :])
                if t % 4 == 3:
                    last.then_inc(transposed, 1)
            pe.wait_ge(evacuated, 4)
            for n in range(OWN):
                nc.tensor.matmul(bank_of(n), wT[:, (n // 2) * C:(n // 2 + 1) * C], xT[:, (n % 2) * BANK:(n % 2 + 1) * BANK],
                                 start=True, stop=True).then_inc(block_ready, 1)
            for t in range(TT):
                last = nc.tensor.matmul(O[:, t // 4, (t % 4) * P:(t % 4 + 1) * P], xT[:, t * P:(t + 1) * P],
                                        wT[:, 2 * C:3 * C], start=True, stop=True)
            last.then_inc(v_self, 1)
            for b in range(CBLOCKS):
                if b >= 2:
                    pe.wait_ge(block_read, b - 1)
                for i in range(block_tiles(b)):
                    t = 4 * b + i
                    if t == CT:
                        pe.wait_ge(tail_in, 32)
                    elif t % STAGE == 0 or i == 0:
                        pe.wait_ge(ctx_in_part[t // STAGE], 16)
                    src = ctx_sb[:, t, 0:C] if t < CT else tail[:, 0:C]
                    last = nc.tensor.transpose(S[:, b % 6, i * P:(i + 1) * P], src, ident[:, :])
                last.then_inc(block_ready, 1)
            pe.wait_ge(kmax_done, 1)
            pe.wait_ge(qabs_done, 3)
            pe.wait_ge(v_self_out, 2)
            for half in range(2):
                last = nc.tensor.matmul(O[0:HEADS, half, :], blk_k[:, :], qsc[:, half * BANK:(half + 1) * BANK],
                                        start=True, stop=True)
            last.then_inc(bound_done, 1)
            pe.wait_ge(block_read, BLOCKS)
            pe.wait_ge(mp_out, 16)
            for i in range(WARM):
                nc.tensor.matmul(S[:, 5, 0:P], ident[:, :], ident[:, :], start=True, stop=True)
            attention_pe(pe, 0)
            spread_sums_pe(pe, 0)

            pe.wait_ge(flag_done, 1)
            redo = pe.value_load(lflag[0:1, 0:1], min_val=0, max_val=1)
            with pe.If(redo > 0):
                with pe.Fori(0, UNITS) as u:
                    with pe.Fori(0, NT) as t:
                        pe.wait_ge(fb_k, u * NT + t + 1)
                        for j in range(GH):
                            r = slice(64 * (j % 2), 64 * (j % 2) + SHIFT)
                            last = nc.tensor.matmul(S[:, j, :], kring[r, 0, j // 2, 0:P], qbuf[r, 0, j // 2, :],
                                                    start=True, stop=True)
                        last.then_inc(fb_s, 1)
                attention_pe(pe, 1)
                spread_sums_pe(pe, 1)
                pe.wait_ge(normed, 2)

            pe.wait_ge(normed, 1)
            pe.wait_ge(wps_in, 16 * GH)
            pe.wait_ge(small_in, 16 * (4 + FFC))
            pe.wait_ge(consts_done, 1)
            for t in range(TT):
                bank = O[:, t // 4, (t % 4) * P:(t % 4 + 1) * P]
                for g in range(GROUPS):
                    nc.tensor.matmul(bank, U[:, g, t * P:(t + 1) * P], wps[:, g, :], start=(g == 0), stop=False)
                last = nc.tensor.matmul(bank, ones1[:, :], brow[:, :], start=False, stop=True)
                if t % 4 == 3:
                    last.then_inc(proj_done, 1)
            for t in range(TT):
                pe.wait_ge(x2n_done, t + 1)
                last = nc.tensor.transpose(S[:, t // 4, (t % 4) * P:(t % 4 + 1) * P], xn[:, t, :], ident[:, :])
                if t % 4 == 3:
                    last.then_inc(transposed2, 1)
            pe.wait_ge(evacuated2, 2)
            for t in range(TT):
                last = nc.tensor.matmul(S[:, 2, t * EXPERTS:(t + 1) * EXPERTS], xT[:, t * P:(t + 1) * P], gw_sb[:, :],
                                        start=True, stop=True)
            last.then_inc(logits_ready, 1)
            pe.wait_ge(shifted_logits, 1)
            pe.wait_ge(b2_in, 16)

            down_banks = [O[:, 0, 0:C], O[:, 1, 0:C], S[:, 4, 0:C], S[:, 5, 0:C]]
            with pe.Fori(0, EXPERTS // 2) as pair:
                for k in range(2):
                    e = pair * 2 + k
                    pe.wait_ge(expert_in[k], pair * 32 + 32)
                    for half in range(2):
                        for f in range(FFC):
                            pe.wait_ge(gelu_done, e * 8 + (4 * half + f - 3 + GB))
                            nc.tensor.matmul(S[:, f, :], w1_sb[:, k, f * P:(f + 1) * P],
                                             xT[:, half * BANK:(half + 1) * BANK], start=True, stop=True).then_inc(hidden_ready, 1)
                    for half in range(2):
                        pe.wait_ge(gelu_done, e * 8 + (4 * half + 4 + GB))
                        for i in range(4):
                            pe.wait_ge(y_added, e * 8 + (4 * half + i - 3 + YB))
                            for f in range(FFC):
                                nc.tensor.matmul(down_banks[i], hT[:, half, f, i * P:(i + 1) * P], w2_sb[:, k, f, :],
                                                 start=(f == 0), stop=False)
                            nc.tensor.matmul(down_banks[i], ones1[:, :], b2row[:, bass.ds(e, 1), :], start=False, stop=True).then_inc(y_ready, 1)

        def attention_act(act, base):
            def exps(half, t, u, step=0):
                act.wait_ge(probs_used, u * NT + (t - 1 + PB) + step * STEP)
                ps = (NT * half + t) % 2
                for a in range(2):
                    slot = (ACTS * half + 2 * t + a) % 3
                    act.wait_ge(scores_ready, u * ACTS + (2 * t + a + 1 + SB) + step * 2 * STEP)
                    nc.scalar.activation(probs[:, ps, 2 * a:2 * a + 2, :], S[:, 2 * slot:2 * slot + 2, :],
                                         ACT.Exp).then_inc(exp_done, 1)

            with act.Fori(0, GROUPS) as g:
                for half in range(2):
                    u = g * 2 + (UNITS * base + half)
                    with act.Fori(0, STEPS) as i:
                        for t in range(STEP):
                            exps(half, t, u, i)
                    for t in range(STEPS * STEP, NT):
                        exps(half, t, u)

        @block.scalar
        def _(act):
            act.sem_inc(exp_done, EB)
            act.sem_inc(gelu_done, GB)
            act.wait_ge(ln_stats, 1)
            nc.scalar.activation(std[:, :], mv[:, :, 1], ACT.Sqrt).then_inc(std_done, 1)
            act.wait_ge(transposed, 1)
            nc.scalar.activation(wT[:, :], O[:, 0, 0:3 * C], ACT.Copy).then_inc(evacuated, 1)
            nc.scalar.activation(wpT_sb[:, :], O[:, 0, 3 * C:4 * C], ACT.Copy).then_inc(evacuated, 1)
            act.wait_ge(evacuated, 2)
            act.sem_inc(wpt_ready, 1)
            for half in range(2):
                act.wait_ge(transposed, 2 + half)
                nc.scalar.activation(xT[:, half * BANK:(half + 1) * BANK], S[:, half, :], ACT.Copy).then_inc(evacuated, 1)

            def part1(n):
                act.wait_ge(block_ready, n + 1)
                if n >= 2:
                    act.wait_ge(parts_out[n % 2], 16 * (n // 2))
                src = bank_of(n)
                if n < 2:
                    q = qsc[:, n * BANK:(n + 1) * BANK]
                    nc.scalar.activation(q, src, ACT.Copy, scale=SCALE).then_inc(qabs_done, 1)
                    act.wait_ge(qabs_done, n + 1)
                    src = q
                nc.scalar.activation(parts[:, n % 2, 0, 0:width(n)], src, ACT.Copy).then_inc(part1_done, 1)

            part1(0)
            for n in range(BLOCKS):
                if n + 1 < BLOCKS:
                    part1(n + 1)
                act.wait_ge(rest_done, n + 1)
                nc.scalar.activation(parts[:, n % 2, 1, 0:width(n)], rest[:, n % 2, 0:width(n)], ACT.Copy).then_inc(part2_done, 1)
                if n == 1:
                    nc.scalar.activation(qsc[:, :], qsc[:, :], ACT.Abs).then_inc(qabs_done, 1)
            act.wait_ge(small_in, 16 * (4 + FFC))
            nc.scalar.activation(tg[:, :], gates[:, :], ACT.Tanh).then_inc(act_step, 1)
            act.wait_ge(values_done, 1 + CT // STAGE + 1)
            act.wait_ge(block_read, BLOCKS)
            attention_act(act, 0)
            act.wait_ge(flag_done, 1)
            redo = act.value_load(lflag[0:1, 0:1], min_val=0, max_val=1)
            with act.If(redo > 0):
                act.wait_ge(fb_rows_in, 16 * 6 * UNITS)
                attention_act(act, 1)
                act.wait_ge(normed, 2)
            act.wait_ge(x1_stats, 1)
            nc.scalar.activation(std[:, :], mv[:, :, 1], ACT.Sqrt).then_inc(std2_done, 1)
            for half in range(2):
                act.wait_ge(transposed2, 1 + half)
                nc.scalar.activation(xT[:, half * BANK:(half + 1) * BANK], S[:, half, :], ACT.Copy).then_inc(evacuated2, 1)
            act.wait_ge(shifted_logits, 1)
            nc.scalar.activation(le[:, :, :], lt[:, :, :], ACT.Exp).then_inc(router_exp, 1)
            act.wait_ge(small_in, 16 * (4 + FFC))
            with act.Fori(0, EXPERTS // 2) as pair:
                for k in range(2):
                    e = pair * 2 + k
                    nc.scalar.activation(b1_now[:, k, :], b1_sb[:, :, bass.ds(e, 1)], ACT.Copy).then_inc(bias_done, 1)
                    for half in range(2):
                        act.wait_ge(y_ready, e * 8 + (4 * half - 4 + YB))
                        for f in range(FFC):
                            act.wait_ge(hidden_ready, e * 8 + (4 * half + f + 1))
                            if half == 0 and f == 0:
                                act.wait_ge(bias_done, e + 1)
                            nc.scalar.activation(hT[:, half, f, :], S[:, f, :], ACT.Gelu,
                                                 bias=b1_now[:, k, f:f + 1]).then_inc(gelu_done, 1)

        def layer_norm(dve, link, src, stats_done, std_ready, out_done):
            for t in range(TT):
                last = link(nc.vector.bn_stats(stats[:, t, :], src[:, t, :]), t == TT - 1)
            for t in range(TT):
                last = link(nc.vector.bn_aggr(mv[:, t, :], stats[:, t, :]), t == TT - 1)
            nc.vector.tensor_scalar(mv[:, :, 1], mv[:, :, 1], EPS, None, ALU.add).then_inc(stats_done, 1)
            dve.wait_ge(std_ready, 1)
            link(nc.vector.reciprocal(rstd[:, :], std[:, :]))
            for t in range(TT):
                nc.vector.tensor_scalar(xn[:, t, :], src[:, t, :], mv[:, t, 0:1], rstd[:, t:t + 1],
                                        ALU.subtract, ALU.mult).then_inc(out_done, 1)

        def copy(dst, src):
            return nc.vector.tensor_scalar(dst, src, 1.0, None, ALU.mult)

        def attention_dve(dve, base):
            def chunk(c, unit, step=0, start=False):
                u, pair0, g = UNITS * base + unit, 2 * (unit // 2 % 2), unit // 2
                w = min(CHUNK, NT - CHUNK * c) * P
                tiles = CHUNK * (CHUNKS - 1) - NT if start and c == 0 else CHUNK * (c - 1)
                if u or not start:
                    dve.wait_ge(scores_ready, u * ACTS + (2 * tiles + SB) + step * 2 * STEP)
                copy(kring[:, c % 2, :, 0:w],
                     kst[:, pair0:pair0 + 2, bass.ds(step * (STEP * P) + c * CHUNK * P, w)]).then_inc(k_ready, 1)
                if u or not start:
                    dve.wait_ge(probs_used, u * NT + (tiles + PB) + step * STEP)
                copy(vring[:, c % 2, 0:w // P, :, 0:D + 1],
                     vres[:, bass.ds(step * STEP + c * CHUNK, w // P), g * GH:(g + 1) * GH, :]).then_inc(v_ready, 1)

            def copy_out(unit):
                dve.wait_ge(probs_used, (UNITS * base + unit + 1) * NT + PB)
                nc.vector.tensor_copy(U[:, unit // 2, (unit % 2) * HALF:(unit % 2 + 1) * HALF],
                                      O[:, unit % 2, :]).then_inc(o_copied, 1)

            for unit in range(UNITS):
                g, half = unit // 2, unit % 2
                if half == 0:
                    dve.wait_ge(k_stack_in, 16 * LOADS * (2 * GROUPS * base + g + 1))
                nc.vector.tensor_copy(qbuf[:, half, :, :],
                                      qst[:, 2 * g:2 * g + 2, half * HALF:(half + 1) * HALF]).then_inc(q_ready, 1)
                chunk(0, unit, start=True)
                chunk(1, unit, start=True)
                if unit:
                    copy_out(unit - 1)
                with dve.Fori(1, STEPS) as i:
                    chunk(0, unit, i)
                    chunk(1, unit, i)
                for c in range(2 * STEPS, CHUNKS):
                    chunk(c, unit)
            copy_out(UNITS - 1)

        def normalise_dve(dve, base):
            for i in range(UNITS):
                dve.wait_ge(l_ready, UNITS * base + i + 1)
                nc.vector.tensor_reduce(lmin[:, i:i + 1], S[:, i % 2, :], axis=AX.X, op=ALU.min).then_inc(dve_step, 1)
                nc.vector.reciprocal(linv[:, i % 2, :], S[:, i % 2, :]).then_inc(linv_done, 1)
                dve.wait_ge(linv_done, UNITS * base + i + 1)
                u_part = U[:, i // 2, (i % 2) * HALF:(i % 2 + 1) * HALF]
                last = nc.vector.tensor_tensor(u_part, u_part, linv[:, i % 2, :], ALU.mult)
                if i == UNITS - 1:
                    last.then_inc(normed, 1)

        @block.vector
        def _(dve):
            steps = [0]

            def link(ins, wait=True):
                steps[0] += 1
                ins.then_inc(dve_step, 1)
                if wait:
                    dve.wait_ge(dve_step, steps[0])

            dve.wait_ge(x_in, 16)
            layer_norm(dve, link, xs, ln_stats, std_done, xn_done)

            def part3(n):
                w = width(n)
                dve.wait_ge(part2_done, n + 1)
                nc.vector.tensor_tensor(parts[:, n % 2, 2, 0:w], rest[:, n % 2, 0:w], parts[:, n % 2, 1, 0:w],
                                        ALU.subtract).then_inc(part3_done, 1)

            for n in range(BLOCKS):
                w = width(n)
                dve.wait_ge(part1_done, n + 1)
                if n >= 2:
                    dve.wait_ge(part3_done, n - 1)
                src = bank_of(n) if n >= 2 else qsc[:, n * BANK:(n + 1) * BANK]
                last = nc.vector.tensor_tensor(rest[:, n % 2, 0:w], src, parts[:, n % 2, 0, 0:w], ALU.subtract)
                last.then_inc(rest_done, 1)
                if n >= 2:
                    nc.vector.tensor_reduce(kabs[:, n - 2:n - 1], src, axis=AX.X, op=ALU.max,
                                            apply_absolute_value=True).then_inc(block_read, 1)
                else:
                    dve.wait_ge(rest_done, n + 1)
                    dve.sem_inc(block_read, 1)
                if n >= 1:
                    part3(n - 1)
                if n == 4:
                    dve.wait_ge(v_self, 1)
                    for half in range(2):
                        nc.vector.tensor_copy(vres[:, 4 * half:4 * half + 4, :, 0:D],
                                              O[:, half, :].rearrange("p (t h d) -> p t h d", h=HEADS, d=D)).then_inc(v_self_out, 1)
            dve.wait_ge(block_read, BLOCKS)
            link(nc.vector.tensor_reduce(kmax[:, :], kabs[:, 0:BLOCKS - 2], axis=AX.X, op=ALU.max))
            nc.vector.tensor_scalar(blk_k[:, :], blk[:, :], kmax[:, 0:1], None, ALU.mult).then_inc(kmax_done, 1)
            part3(BLOCKS - 1)
            dve.wait_ge(bound_done, 1)
            dve.wait_ge(part3_done, BLOCKS)
            dve.wait_ge(parts_out[0], 16 * ((BLOCKS + 1) // 2))
            dve.wait_ge(parts_out[1], 16 * (BLOCKS // 2))
            m3 = [mparts.rearrange("h s i k -> h (s i k)")[:, i * TOKENS:(i + 1) * TOKENS].rearrange(
                "h (s k) -> h s k", s=2) for i in range(3)]
            link(nc.vector.tensor_scalar(mneg, O[0:HEADS, :, :], -BOUND_SLACK, -BOUND_MAX, ALU.mult, ALU.max))
            link(nc.vector.tensor_copy(m3[0], mneg))
            link(nc.vector.tensor_tensor(mrem, mneg, m3[0], ALU.subtract))
            link(nc.vector.tensor_copy(m3[1], mrem))
            nc.vector.tensor_tensor(m3[2], mrem, m3[1], ALU.subtract).then_inc(bound_parts, 1)

            dve.sem_inc(o_copied, OB)
            dve.sem_inc(y_added, YB)
            dve.wait_ge(consts_done, 1)
            dve.wait_ge(values_done, 1 + CT // STAGE + 1)
            dve.wait_ge(v_self_out, 2)
            dve.wait_ge(q_stack_in, 16 * (LOADS + 2))
            attention_dve(dve, 0)
            normalise_dve(dve, 0)
            steps[0] += UNITS
            dve.wait_ge(dve_step, steps[0])
            link(nc.vector.tensor_reduce(kmax[:, :], lmin[:, :], axis=AX.X, op=ALU.min))
            nc.vector.tensor_scalar(lneg[:, :], kmax[:, :], -1.0, None, ALU.mult).then_inc(lneg_done, 1)
            dve.wait_ge(lall_done, 1)
            nc.vector.tensor_scalar(lflag[:, :], lall[:, :], -L_MIN, None, ALU.is_gt).then_inc(flag_done, 1)
            dve.wait_ge(flag_done, 1)
            redo = dve.value_load(lflag[0:1, 0:1], min_val=0, max_val=1)
            with dve.If(redo > 0):
                with dve.Fori(0, GROUPS // 2) as gg:
                    for parity in range(2):
                        g = gg * 2 + parity
                        dve.wait_ge(k_stack_in, gg * (2 * 16 * LOADS) + 16 * LOADS * (GROUPS + parity + 1))
                        for half in range(2):
                            u = gg * 4 + (2 * parity + half)
                            copy(qbuf[:, 0, :, :], qst[:, bass.ds(g * 2, 2), half * HALF:(half + 1) * HALF]).then_inc(fb_m, 1)
                            nc.vector.memset(runmax, -3.0e38).then_inc(fb_m, 1)
                            with dve.Fori(0, NT) as t:
                                copy(kring[:, 0, :, 0:P],
                                                      kst[:, 2 * parity:2 * parity + 2, bass.ds(t * P, P)]).then_inc(fb_k, 1)
                                dve.wait_ge(fb_s, u * NT + t + 1)
                                dve.wait_ge(fb_m, u * (NT + 2) + t + 2)
                                nc.vector.tensor_tensor(runmax, runmax, S[:, 0:4, :], ALU.max).then_inc(fb_m, 1)
                                dve.wait_ge(fb_m, u * (NT + 2) + t + 3)
                            nc.vector.memset(mrest, 0.0).then_inc(fb_max, 1)
                            dve.wait_ge(fb_all, u + 1)
                            dve.wait_ge(fb_rows_in, u * 96)
                            nc.vector.tensor_scalar(mrow, allmax[0:1, :], -1.0, None, ALU.mult).then_inc(fb_neg, 1)
                            dve.wait_ge(fb_neg, u * 4 + 1)
                            nc.vector.tensor_copy(rowparts[:, 0, :], mrow).then_inc(fb_neg, 1)
                            dve.wait_ge(fb_neg, u * 4 + 2)
                            nc.vector.tensor_tensor(mrest, mrow, rowparts[:, 0, :], ALU.subtract).then_inc(fb_neg, 1)
                            dve.wait_ge(fb_neg, u * 4 + 3)
                            nc.vector.tensor_copy(rowparts[:, 1, :], mrest).then_inc(fb_neg, 1)
                            dve.wait_ge(fb_neg, u * 4 + 4)
                            nc.vector.tensor_tensor(rowparts[:, 2, :], mrest, rowparts[:, 1, :], ALU.subtract).then_inc(fb_rows, 1)
                            dve.wait_ge(fb_rows, u + 1)
                            dve.sem_inc(fb_units, 1)
                dve.wait_ge(fb_rows_in, 96 * UNITS)
                attention_dve(dve, 1)
                normalise_dve(dve, 1)
                dve.wait_ge(normed, 2)

            dve.wait_ge(act_step, 1)
            for half in range(2):
                dve.wait_ge(proj_done, half + 1)
                rows = xs[:, 4 * half:4 * half + 4, :]
                nc.vector.scalar_tensor_tensor(out=rows, in0=O[:, half, :].rearrange("p (t c) -> p t c", t=4), scalar=tg[:, 0:1],
                                               in1=rows, op0=ALU.mult, op1=ALU.add).then_inc(x1_done, 1)
            dve.wait_ge(x1_done, 2)

            steps2 = [0]

            def second(ins):
                steps2[0] += 1
                ins.then_inc(tail_step, 1)
                dve.wait_ge(tail_step, steps2[0])

            layer_norm(dve, lambda ins, wait=True: second(ins), xs, x1_stats, std2_done, x2n_done)
            dve.wait_ge(logits_ready, 1)
            second(nc.vector.tensor_copy(lg[:, :, :], S[:, 2, 0:TT * EXPERTS].rearrange("p (t e) -> p t e", t=TT)))
            second(nc.vector.tensor_reduce(r1[:, 0, :], lg[:, :, :], axis=AX.X, op=ALU.max))

            def spread(i):
                return r1[:, i, :].rearrange("p (t o) -> p t o", o=1).broadcast_to([P, TT, EXPERTS])

            nc.vector.tensor_tensor(lt[:, :, :], lg[:, :, :], spread(0), ALU.subtract).then_inc(shifted_logits, 1)
            dve.wait_ge(shifted_logits, 1)
            second(nc.vector.tensor_scalar(cand[:, :, :], lt[:, :, :], 0.0, float(EXPERTS), ALU.is_lt, ALU.mult))
            second(nc.vector.tensor_tensor(cand[:, :, :], cand[:, :, :], iota8[:, :, :], ALU.add))
            second(nc.vector.tensor_reduce(r1[:, 1, :], cand[:, :, :], axis=AX.X, op=ALU.min))
            second(nc.vector.tensor_tensor(cand[:, :, :], cand[:, :, :], spread(1), ALU.is_equal))
            dve.wait_ge(router_exp, 1)
            second(nc.vector.tensor_reduce(r1[:, 2, :], le[:, :, :], axis=AX.X, op=ALU.add))
            second(nc.vector.reciprocal(r1[:, 3, :], r1[:, 2, :]))
            second(nc.vector.tensor_tensor(cand[:, :, :], cand[:, :, :], spread(3), ALU.mult))
            second(nc.vector.tensor_scalar(rw[:, :, :], cand[:, :, :], tg[:, 1:2], None, ALU.mult))
            down_banks = [O[:, 0, 0:C], O[:, 1, 0:C], S[:, 4, 0:C], S[:, 5, 0:C]]
            with dve.Fori(0, EXPERTS) as e:
                for t in range(TT):
                    dve.wait_ge(y_ready, e * 8 + (t + 1 + YB))
                    dve.wait_ge(y_added, e * 8 + (t - 7 + YB))
                    nc.vector.scalar_tensor_tensor(out=xs[:, t, :], in0=down_banks[t % 4], scalar=rw[:, t, bass.ds(e, 1)],
                                                   in1=xs[:, t, :], op0=ALU.mult, op1=ALU.add).then_inc(y_added, 1)


_INS = ['x', 'ctx_2048', 'g_xattn', 'g_ffn', 'L0_xattn_w_qkv', 'L0_xattn_w_proj', 'L0_xattn_b_proj',
        'L0_ffn_gate_w', 'L0_ffn_w1', 'L0_ffn_b1', 'L0_ffn_w2', 'L0_ffn_b2']


def kernel(**inputs):
    import numpy as _np
    import concourse.bacc as _bacc
    from concourse import mybir as _mybir
    from concourse.bass_utils import run_bass_kernel_spmd as _run

    nc = _bacc.Bacc("TRN2", target_bir_lowering=False, num_devices=1)
    arrays, args = {}, []
    for name in _INS:
        a = _np.ascontiguousarray(inputs[name])
        arrays[f"in_{name}_dram"] = a
        args.append(nc.dram_tensor(f"in_{name}_dram", a.shape, _mybir.dt.from_np(a.dtype), kind="ExternalInput").ap())
    args.append(nc.dram_tensor("out_0_dram", (1, TOKENS, C), _mybir.dt.float32, kind="ExternalOutput").ap())
    for name, shape, dt in (("k_parts", (3, P, KEYS), BF16), ("q_parts", (3, P, TOKENS), BF16),
                            ("bound_rows", (3, HEADS, TOKENS), BF16), ("proj_t", (P, C), F32)):
        args.append(nc.dram_tensor(name, shape, dt).ap())
    program(nc, *args)
    r = _run(nc, [arrays], core_ids=[0])
    return r.results[0]["out_0_dram"]
```

```python
from contextlib import ExitStack

import concourse.bass as bass
from concourse import mybir

F32 = mybir.dt.float32
BF16 = mybir.dt.bfloat16
I32 = mybir.dt.int32
ALU = mybir.AluOpType
ACT = mybir.ActivationFunctionType
AX = mybir.AxisListType

P = 128
BANK = 512

TOKENS, C = 1024, 128
CTX = 6404
HEADS, D = 16, 8
EXPERTS, FF = 8, 512
FFC = FF // P
TT = TOKENS // P
HALF = BANK
GROUPS = 4
GH = HEADS // GROUPS
PAIRS = HEADS // 2

CT = CTX // P
REST = CTX - CT * P
NT = TT + CT + 1
KEYS = NT * P
STAGE = 10

Q_PART = (0, 0, 0, 1, 1, 2)
K_PART = (0, 1, 2, 0, 1, 0)
SLOTS = len(Q_PART)
SHIFT = SLOTS * D
ROWS = SHIFT + 3

CHUNK = 3
CHUNKS = (NT + CHUNK - 1) // CHUNK
STEP = 2 * CHUNK
STEPS = NT // STEP
TAKE = 2
BANKS = GH * (NT - 1) + 1
EXPS = (BANKS + TAKE - 1) // TAKE
CHUNK_EXPS = GH * CHUNK // TAKE
S_BANKS, P_BANKS = 6, 12
UNITS = 2 * GROUPS

SB, EB, PB, OB, LB, GB, YB = 8, 3, 4, 2, 2, 4, 8

WARM = 16
SMALL = 16 * 5

SCALE = float(D) ** -0.5
EPS = 1e-5
L_MIN = 2.0 ** -60
BOUND_SLACK = 1.0 + 2.0 ** -10
BOUND_MAX = 1.0e38
ONES_PAIR = 0x3F803F80


def program(nc, x, ctx_in, g_xattn, g_ffn, w_qkv, w_proj, b_proj, gate_w, w1, b1, w2, b2, out, kp, qp, mp, wpt):
    with ExitStack() as st:
        def sb(name, shape, dt=F32):
            return st.enter_context(nc.sbuf_tensor(name, shape, dt))

        def psum(name, shape, dt=F32):
            return st.enter_context(nc.psum_tensor(name, shape, dt))

        def sem(name):
            return st.enter_context(nc.semaphore(name))

        S = psum("S", [P, 6, BANK])
        O = psum("O", [P, 2, BANK])

        kst = sb("kst", [P, 4, KEYS], BF16)
        vres = sb("vres", [P, NT - 1, HEADS, D + 1])
        vlast = sb("vlast", [P, GROUPS, P])
        vlast_now = sb("vlast_now", [P, P])
        qst = sb("qst", [P, PAIRS, TOKENS], BF16)
        work = sb("work", [P, 26 * BANK])
        ctx_sb = work[:, 0:CT * 2 * C].rearrange("p (t c) -> p t c", c=2 * C)
        probs = work[:, 0:P_BANKS * BANK].rearrange("p (b q) -> p b q", b=P_BANKS)
        Uraw = work[:, 12 * BANK:14 * BANK].rearrange("p (s q) -> p s q", s=2)
        U = work[:, 14 * BANK:14 * BANK + GROUPS * TOKENS].rearrange("p (g q) -> p g q", g=GROUPS)
        hT = work[:, 0:2 * FFC * BANK].rearrange("p (s f q) -> p s f q", s=2, f=FFC)
        w1_sb = work[:, 22 * BANK:22 * BANK + 2 * FF].rearrange("p (s f) -> p s f", s=2)
        w2_sb = work[:, 24 * BANK:24 * BANK + 2 * FFC * C].rearrange("p (s f c) -> p s f c", s=2, f=FFC)
        runmax = work[:, 0:4 * BANK].rearrange("p (h q) -> p h q", h=4)
        allmax = work[:, 4 * BANK:8 * BANK]
        mrow = work[0:1, 8 * BANK:12 * BANK]
        mrest = work[0:1, 4 * BANK:8 * BANK]
        rowparts = work[0:1, 12 * BANK:18 * BANK].bitcast(BF16).rearrange("p (i q) -> p i q", i=3)
        tail = sb("tail", [P, C])
        kring = sb("kring", [P, 2, 2, CHUNK * P], BF16)
        vring = sb("vring", [P, 2, CHUNK, GH, 32])
        qbuf = sb("qbuf", [P, 2, 2, HALF], BF16)
        xs = sb("xs", [P, TT, C])
        xn = sb("xn", [P, TT, C])
        xT = sb("xT", [P, TOKENS])
        qsc = xn[:, :, :].rearrange("p t c -> p (t c)")
        rest = sb("rest", [P, 2, BANK])
        parts = sb("parts", [P, 2, 3, BANK], BF16)
        part_slots = [parts[:, 0, :, :], parts[:, 1, :, :],
                      kring[:, :, :, :].rearrange("p a b k -> p (a b k)").rearrange("p (i k) -> p i k", i=3),
                      qbuf[:, :, :, :].rearrange("p a b k -> p (a b k)")[:, 0:3 * BANK].rearrange("p (i k) -> p i k", i=3)]
        mneg = rest[0:HEADS, :, :]
        mrem = qsc[0:HEADS, :].rearrange("p (s q) -> p s q", s=2)
        mparts = work[0:HEADS, 14 * BANK:17 * BANK].bitcast(BF16).rearrange("h (i k) -> h i k", i=3)
        wq_sb = sb("wq_sb", [P, 3, C])
        wT = sb("wT", [P, 3 * C])
        wp_sb = sb("wp_sb", [P, C])
        wpT_sb = sb("wpT_sb", [P, C])
        wps = sb("wps", [P, GROUPS, C])
        ident = sb("ident", [P, P])
        blk = sb("blk", [P, HEADS])
        blk_k = sb("blk_k", [P, HEADS])
        selL = sb("selL", [P, P])
        ones1 = sb("ones1", [1, P])
        brow = sb("brow", [1, C])
        b2_sb = sb("b2_sb", [EXPERTS, C])
        rwT = xn[0:EXPERTS, :, :].rearrange("e t c -> e (t c)")
        b1_now = sb("b1_now", [P, 2, FFC])
        gw_sb = sb("gw_sb", [P, EXPERTS])
        gates = sb("gates", [P, 2])
        tg = sb("tg", [P, 2])
        unread = sb("unread", [P, 2])
        stats = sb("stats", [P, TT, 6])
        mv = sb("mv", [P, TT, 2])
        std = sb("std", [P, TT])
        rstd = sb("rstd", [P, TT])
        kabs = sb("kabs", [P, 16])
        kmax = sb("kmax", [P, 1])
        lmin = sb("lmin", [P, UNITS])
        lneg = sb("lneg", [P, 1])
        lall = sb("lall", [P, 1])
        lflag = sb("lflag", [P, 1], I32)
        lg = sb("lg", [P, TT, EXPERTS])
        lt = sb("lt", [P, TT, EXPERTS])
        le = sb("le", [P, TT, EXPERTS])
        cand = sb("cand", [P, TT, EXPERTS])
        iota8 = sb("iota8", [P, TT, EXPERTS])
        rw = sb("rw", [P, TT, EXPERTS])
        r1 = sb("r1", [P, 4, TT])
        linv = rest

        x_in = sem("x_in")
        w_in = sem("w_in")
        small_in = sem("small_in")
        tail_in = sem("tail_in")
        pool_step = sem("pool_step")
        consts_done = sem("consts_done")
        wps_zero = sem("wps_zero")
        values_done = sem("values_done")
        last_ones = sem("last_ones")
        last_values_in = sem("last_values_in")
        ln_stats = sem("ln_stats")
        std_done = sem("std_done")
        xn_done = sem("xn_done")
        transposed = sem("transposed")
        evacuated = sem("evacuated")
        v_self = sem("v_self")
        v_self_out = sem("v_self_out")
        block_ready = sem("block_ready")
        part1_done = sem("part1_done")
        rest_done = sem("rest_done")
        block_read = sem("block_read")
        part2_done = sem("part2_done")
        part3_done = sem("part3_done")
        kmax_done = sem("kmax_done")
        qabs_done = sem("qabs_done")
        bound_done = sem("bound_done")
        bound_parts = sem("bound_parts")
        mp_out = sem("mp_out")
        q_stack_in = sem("q_stack_in")
        k_stack_in = sem("k_stack_in")
        wpt_ready = sem("wpt_ready")
        wpt_out = sem("wpt_out")
        wps_in = sem("wps_in")
        scores_ready = sem("scores_ready")
        exp_done = sem("exp_done")
        probs_used = sem("probs_used")
        k_ready = sem("k_ready")
        v_ready = sem("v_ready")
        q_ready = sem("q_ready")
        o_copied = sem("o_copied")
        l_ready = sem("l_ready")
        linv_done = sem("linv_done")
        normed = sem("normed")
        dve_step = sem("dve_step")
        act_step = sem("act_step")
        lneg_done = sem("lneg_done")
        lall_done = sem("lall_done")
        flag_done = sem("flag_done")
        proj_done = sem("proj_done")
        x1_stats = sem("x1_stats")
        std2_done = sem("std2_done")
        x2n_done = sem("x2n_done")
        transposed2 = sem("transposed2")
        evacuated2 = sem("evacuated2")
        logits_ready = sem("logits_ready")
        shifted_logits = sem("shifted_logits")
        router_exp = sem("router_exp")
        hidden_ready = sem("hidden_ready")
        gelu_done = sem("gelu_done")
        y_ready = sem("y_ready")
        y_added = sem("y_added")
        out_written = sem("out_written")
        fb_k = sem("fb_k")
        fb_s = sem("fb_s")
        fb_m = sem("fb_m")
        fb_max = sem("fb_max")
        fb_all = sem("fb_all")
        fb_rows = sem("fb_rows")
        fb_rows_in = sem("fb_rows_in")
        fb_units = sem("fb_units")
        fb_neg = sem("fb_neg")
        rw_done = sem("rw_done")
        bn_done = sem("bn_done")
        aggregated = sem("aggregated")
        rwT_ready = sem("rwT_ready")
        rwT_copied = sem("rwT_copied")
        b2_ready = sem("b2_ready")
        b2_added = sem("b2_added")
        uraw_set = sem("uraw_set")
        x1_done = sem("x1_done")
        tail_step = sem("tail_step")
        ctx_keys_in = [sem(f"ctx_keys_in{i}") for i in range(CT // STAGE)]
        ctx_values_in = [sem(f"ctx_values_in{i}") for i in range(CT // STAGE)]
        parts_out = [sem(f"parts_out{i}") for i in range(4)]
        expert_in = [sem("expert_in0"), sem("expert_in1")]

        block = st.enter_context(nc.Block())

        CBLOCKS = (CT + 1 + 3) // 4
        ORDER = ([("c", b) for b in range(4)] + [("q", 0), ("q", 1), ("k", 0), ("k", 1)]
                 + [("c", b) for b in range(4, CBLOCKS)])
        BLOCKS = len(ORDER)

        VALUES_AT = (6, 8, 10, 12, 14)

        def block_tiles(b):
            return min(4, CT + 1 - 4 * b)

        def width(n):
            return block_tiles(ORDER[n][1]) * P if ORDER[n][0] == "c" else BANK

        def bank_of(n):
            return S[:, n % 6, 0:width(n)]

        def outs(n):
            return 16 * (n // 4)

        ctx_main = ctx_in[0, 0:CT * P, :].rearrange("(p t) c -> p t c", t=CT)
        K_LOADS = 2 * SLOTS
        K_CUTS = (0, 24 * P, KEYS)
        FIRST_LOADS = K_LOADS * (len(K_CUTS) - 1)

        def stacks_in(number):
            return 16 * (FIRST_LOADS + K_LOADS * number)

        def load_keys(sp, group, k0, k1, parities=range(2), slots=range(SLOTS)):
            b = 2 * (group % 2)
            for par in parities:
                for slot in slots:
                    heads = kp[K_PART[slot], GH * group:GH * (group + 1), :, k0:k1].rearrange("(w a) d k -> a d w k", a=2)[par]
                    r = 64 * par + D * slot
                    sp.dma_start(kst[r:r + D, b:b + 2, k0:k1], heads).then_inc(k_stack_in, 16)

        def load_queries(sp, par, slots):
            for slot in slots:
                r = 64 * par + D * slot
                sp.dma_start(qst[r:r + D, :, :], qp[Q_PART[slot]].rearrange("(w a) d k -> a d w k", a=2)[par]).then_inc(q_stack_in, 16)

        @block.sync
        def _(sp):
            sp.dma_start(xs[:, :, :], x.rearrange("a (p t) c -> p (a t) c", t=TT)).then_inc(x_in, 16)
            sp.dma_start(wq_sb[:, :, :], w_qkv.rearrange("(t p) c -> p t c", p=P)).then_inc(w_in, 16)
            sp.dma_start(wp_sb[:, :], w_proj).then_inc(w_in, 16)
            for i in range(CT // STAGE):
                tiles = slice(i * STAGE, (i + 1) * STAGE)
                sp.dma_start(ctx_sb[:, tiles, 0:C], ctx_main[:, tiles, 0:C]).then_inc(ctx_keys_in[i], 16)
            sp.dma_start(tail[0:REST, :], ctx_in[0, CT * P:CTX, 0:C]).then_inc(tail_in, 16)
            sp.dma_start(tail[REST:P, :], ctx_in[0, CTX - 1:CTX, 0:C].broadcast_to([P - REST, C])).then_inc(tail_in, 16)
            sp.dma_start(gates[:, 0:1], g_xattn.rearrange("(a b) -> a b", a=1).broadcast_to([P, 1])).then_inc(small_in, 16)
            sp.dma_start(gates[:, 1:2], g_ffn.rearrange("(a b) -> a b", a=1).broadcast_to([P, 1])).then_inc(small_in, 16)
            sp.dma_start(brow[:, :], b_proj.rearrange("(a c) -> a c", a=1)).then_inc(small_in, 16)
            sp.dma_start(b2_sb[:, :], b2).then_inc(small_in, 16)
            sp.dma_start(gw_sb[:, :], gate_w).then_inc(small_in, 16)
            for n, (what, i) in enumerate(ORDER):
                if n < CT // STAGE:
                    tiles = slice(n * STAGE, (n + 1) * STAGE)
                    sp.dma_start(ctx_sb[:, tiles, C:2 * C], ctx_main[:, tiles, C:2 * C]).then_inc(ctx_values_in[n], 16)
                sp.wait_ge(part3_done, n + 1)
                w = width(n)
                k0 = i * BANK if what != "c" else TOKENS + i * BANK
                dst = (qp if what == "q" else kp).rearrange("i h d k -> (h d) i k")
                sp.dma_start(dst[:, :, k0:k0 + w], part_slots[n % 4][:, :, 0:w]).then_inc(parts_out[n % 4], 16)
                if n == 8:
                    sp.wait_ge(consts_done, 2)
                    for slot in range(2):
                        sp.wait_ge(parts_out[slot], outs(8 + slot))
                if n == 12:
                    for slot in range(4):
                        sp.wait_ge(parts_out[slot], outs(8 + slot))
                if 8 <= n < 16:
                    par, slots = n // 2 % 2, range(3 * (n % 2), 3 * (n % 2) + 3)
                    if n < 12:
                        load_queries(sp, par, slots)
                    else:
                        load_keys(sp, 0, K_CUTS[0], K_CUTS[1], (par,), slots)
            sp.wait_ge(bound_parts, 2)
            sp.dma_start(mp.rearrange("i h k -> h i k"), mparts).then_inc(mp_out, 16)
            sp.wait_ge(mp_out, 16)
            for par in range(2):
                sp.dma_start(qst[64 * par + SHIFT:64 * par + ROWS, :, :],
                             mp.rearrange("i (w a) k -> a i w k", a=2)[par]).then_inc(q_stack_in, 16)
            for slot in range(4):
                sp.wait_ge(parts_out[slot], outs(BLOCKS - 1 - (BLOCKS - 1 - slot) % 4 + 4))
            sp.wait_ge(k_stack_in, 16 * K_LOADS)
            load_keys(sp, 0, K_CUTS[1], K_CUTS[2])
            sp.wait_ge(last_ones, GH)
            with nc.allow_non_contiguous_dma(reason="2 KB, once"):
                for j in range(GH):
                    sp.dma_start(vlast[32 * j:32 * j + REST, :, 32 * j:32 * j + D],
                                 ctx_in[0, CT * P:CTX, C:2 * C].rearrange("k (g j d) -> j k g d", j=GH, d=D)[j]).then_inc(last_values_in, 16)
            sp.wait_ge(wpt_ready, 1)
            sp.dma_start(wpt, wpT_sb[:, :]).then_inc(wpt_out, 16)
            sp.wait_ge(wpt_out, 16)
            sp.wait_ge(wps_zero, 1)
            for j in range(GH):
                sp.dma_start(wps[32 * j:32 * j + D, :, :],
                             wpt.rearrange("(g j d) c -> j d g c", j=GH, d=D)[j]).then_inc(wps_in, 16)
            sp.wait_ge(values_done, CT // STAGE)
            sp.wait_ge(block_read, BLOCKS)
            def load_expert(e):
                k = e % 2
                sp.dma_start(w1_sb[:, k, :], w1[e]).then_inc(expert_in[k], 16)
                sp.dma_start(w2_sb[:, k, :, :], w2[e].rearrange("(f p) c -> p f c", p=P)).then_inc(expert_in[k], 16)
                with nc.allow_non_contiguous_dma(reason="2 KB of biases"):
                    sp.dma_start(b1_now[:, k, :], b1[e].rearrange("(f p) -> p f", p=P)).then_inc(expert_in[k], 16)

            load_expert(0)
            load_expert(1)

            def load_group(number, group):
                sp.wait_ge(k_stack_in, stacks_in(number - 1))
                load_keys(sp, group, 0, KEYS)

            sp.wait_ge(consts_done, 3)
            for g in range(1, GROUPS):
                if g >= 2:
                    sp.wait_ge(o_copied, OB + 2 * (g - 1))
                load_group(g, g)

            sp.wait_ge(flag_done, 1)
            redo = sp.value_load(lflag[0:1, 0:1], min_val=0, max_val=1)
            with sp.If(redo > 0):
                for g in range(GROUPS):
                    if g >= 2:
                        sp.wait_ge(fb_units, 2 * (g - 1))
                    load_group(GROUPS + g, g)
                    for half in range(2):
                        sp.wait_ge(fb_rows, 2 * g + half + 1)
                        for par in range(2):
                            for i in range(3):
                                r = 64 * par + SHIFT + i
                                heads = rowparts[:, i, :].rearrange("p (w a q) -> p a w q", w=2, a=2)[:, par, :, :]
                                sp.dma_start(qst[r:r + 1, 2 * g:2 * g + 2, half * HALF:(half + 1) * HALF],
                                             heads).then_inc(fb_rows_in, 16)
                for g in range(GROUPS):
                    if g < 2:
                        sp.wait_ge(fb_units, 2 * (g + 3))
                    else:
                        sp.wait_ge(o_copied, OB + UNITS + 2 * (g - 1))
                    load_group(2 * GROUPS + g, g)
                sp.wait_ge(normed, 2 * UNITS)

            for e in range(2, EXPERTS):
                sp.wait_ge(y_ready, YB + 8 * (e - 1))
                sp.wait_ge(expert_in[e % 2], 48 * (e // 2))
                load_expert(e)
            sp.wait_ge(y_added, YB + 8 * EXPERTS)
            sp.dma_start(out.rearrange("a (p t) c -> p (a t) c", t=TT), xs[:, :, :]).then_inc(out_written, 16)
            sp.wait_ge(out_written, 16)

        @block.gpsimd
        def _(pool):
            nc.gpsimd.memset(ident[:, :], 0.0).then_inc(pool_step, 1)
            nc.gpsimd.memset(selL[:, :], 0.0).then_inc(pool_step, 1)
            pool.wait_ge(pool_step, 2)
            nc.gpsimd.affine_select(out=ident[:, :], in_=ident[:, :], compare_op=ALU.not_equal, fill=1.0,
                                    base=0, pattern=[[-1, P]], channel_multiplier=1).then_inc(pool_step, 1)
            sel4 = selL[:, :].rearrange("p (j r) -> p j r", j=GH)
            nc.gpsimd.affine_select(out=sel4, in_=sel4, compare_op=ALU.not_equal, fill=1.0,
                                    base=-D, pattern=[[-32, GH], [0, 32]], channel_multiplier=1).then_inc(pool_step, 1)
            nc.gpsimd.iota(iota8[:, :, :], pattern=[[0, TT], [1, EXPERTS]], base=0, channel_multiplier=0,
                           allow_small_or_imprecise_dtypes=True).then_inc(pool_step, 1)
            nc.gpsimd.memset(kst[:, 0:2, :].bitcast(I32), ONES_PAIR).then_inc(consts_done, 1)
            nc.gpsimd.memset(qst[:, :, :].bitcast(I32), 0).then_inc(consts_done, 1)
            def fill_rest():
                nc.gpsimd.memset(wps[:, :, :], 0.0).then_inc(wps_zero, 1)
                nc.gpsimd.memset(ones1[:, :], 1.0).then_inc(pool_step, 1)
                nc.gpsimd.memset(vring[:, :, :, :, :], 0.0).then_inc(pool_step, 1)
                nc.gpsimd.memset(vres[:, :, :, D:D + 1], 1.0).then_inc(pool_step, 1)
                nc.gpsimd.memset(vlast[:, :, :], 0.0).then_inc(pool_step, 1)
                pool.wait_ge(pool_step, 9)
                for j in range(GH):
                    nc.gpsimd.memset(vlast[32 * j:32 * j + REST, :, 32 * j + D:32 * j + D + 1], 1.0).then_inc(last_ones, 1)

            for n in range(BLOCKS):
                w = width(n)
                pool.wait_ge(part2_done, n + 1)
                if n == 4:
                    pool.wait_ge(last_ones, GH)
                nc.gpsimd.tensor_tensor(part_slots[n % 4][:, 2, 0:w], rest[:, n % 2, 0:w], part_slots[n % 4][:, 1, 0:w],
                                        ALU.subtract).then_inc(part3_done, 1)
                if n == 3:
                    fill_rest()
            nc.gpsimd.memset(kst[:, 2:4, :].bitcast(I32), ONES_PAIR).then_inc(consts_done, 1)
            pool.wait_ge(lneg_done, 1)
            nc.gpsimd.partition_all_reduce(lall[:, :], lneg[:, :], P, bass.bass_isa.ReduceOp.max).then_inc(lall_done, 1)
            pool.wait_ge(flag_done, 1)
            redo = pool.value_load(lflag[0:1, 0:1], min_val=0, max_val=1)
            with pool.If(redo > 0):
                for u in range(UNITS):
                    pool.wait_ge(fb_max, u + 1)
                    nc.gpsimd.partition_all_reduce(allmax, work[:, 0:4 * BANK], P,
                                                   bass.bass_isa.ReduceOp.max).then_inc(fb_all, 1)

        def attention_pe(pe, base):
            def score(half, b):
                t, j, c = b // GH, b % GH, b // GH // CHUNK
                if t == NT - 1:
                    for j in range(GH):
                        r = slice(64 * (j % 2), 64 * (j % 2) + ROWS)
                        last = nc.tensor.matmul(S[32 * j:32 * j + 32, b % S_BANKS, :],
                                                kring[r, c % 2, j // 2, (t % CHUNK) * P:(t % CHUNK) * P + 32],
                                                qbuf[r, half, j // 2, :], start=True, stop=True,
                                                tile_position=(64 * (j % 2), 32 * j))
                    return last
                r = slice(64 * (j % 2), 64 * (j % 2) + ROWS)
                return nc.tensor.matmul(S[:, b % S_BANKS, :], kring[r, c % 2, j // 2, (t % CHUNK) * P:(t % CHUNK + 1) * P],
                                        qbuf[r, half, j // 2, :], start=True, stop=True)

            def scores(half, e, u, step=0):
                first, end = TAKE * e, min(TAKE * (e + 1), BANKS)
                def room(e):
                    pe.wait_ge(exp_done, u * EXPS + (e - S_BANKS // TAKE + 1 + EB) + step * 2 * CHUNK_EXPS)

                if e < EXPS - 1:
                    room(e)
                for b in range(first, end):
                    if e == EXPS - 2 and b == end - 1:
                        room(e + 1)
                    if b % (GH * CHUNK) == 0:
                        pe.wait_ge(k_ready, u * CHUNKS + (b // (GH * CHUNK) + 1) + step * 2)
                    last = score(half, b)
                last.then_inc(scores_ready, 1)

            def values(half, t, u, step=0, start=False):
                c = t // CHUNK
                if t % CHUNK == 0:
                    pe.wait_ge(v_ready, u * CHUNKS + (c + 1) + step * 2)
                pe.wait_ge(exp_done, u * EXPS + (min(GH * t + GH, BANKS) - 1) // TAKE + (1 + EB) + step * 2 * CHUNK_EXPS)
                b = GH * t + half * (P_BANKS // 2)
                for j in range(GH):
                    if t == NT - 1:
                        v, bank = vlast_now[:, 32 * j:32 * j + 32], b % P_BANKS
                    else:
                        v, bank = vring[:, c % 2, t % CHUNK, j, :], (b + j) % P_BANKS
                    last = nc.tensor.matmul(O[32 * j:32 * j + 32, half, :], v, probs[:, bank, :],
                                            start=start, stop=(t == NT - 1), tile_position=(0, 32 * j))
                last.then_inc(probs_used, 1)

            def tile(half, t, u, step=0, start=False):
                scores(half, 2 * t + 2, u, step)
                if 2 * t + 3 < EXPS:
                    scores(half, 2 * t + 3, u, step)
                values(half, t, u, step, start)

            def spread_sums(half, u):
                pe.wait_ge(o_copied, u + (1 + OB))
                nc.tensor.matmul(O[:, half, :], selL[:, :], Uraw[:, half, :], start=True, stop=True).then_inc(l_ready, 1)

            def group(g, last_group):
                for half in range(2):
                    u = g * 2 + (UNITS * base + half)
                    pe.wait_ge(linv_done, u + (LB - 1))
                    for t in range(STEP):
                        tile(half, t, u, start=(t == 0))
                    spread_sums(1 - half, u - 1)
                    with pe.Fori(1, STEPS) as i:
                        for t in range(STEP):
                            tile(half, t, u, i)
                    for t in range(STEPS * STEP, NT - 1):
                        tile(half, t, u)
                    if not (last_group and half == 1):
                        pe.wait_ge(q_ready, u + 2)
                        scores(1 - half, 0, u + 1)
                        scores(1 - half, 1, u + 1)
                    values(half, NT - 1, u)

            pe.wait_ge(q_ready, UNITS * base + 1)
            scores(0, 0, UNITS * base)
            scores(0, 1, UNITS * base)
            with pe.Fori(0, GROUPS - 1) as g:
                group(g, False)
            group(GROUPS - 1, True)
            spread_sums(1, UNITS * base + UNITS - 1)
            pe.wait_ge(normed, UNITS * base + UNITS - 1)
            pe.wait_ge(wps_in, 16 * GH)
            pe.wait_ge(small_in, SMALL)
            pe.wait_ge(pool_step, 9)
            project(0)

        def project(half):
            for t in range(4 * half, 4 * half + 4):
                bank = O[:, half, (t % 4) * P:(t % 4 + 1) * P]
                for g in range(GROUPS):
                    nc.tensor.matmul(bank, U[:, g, t * P:(t + 1) * P], wps[:, g, :], start=(g == 0), stop=False)
                last = nc.tensor.matmul(bank, ones1[:, :], brow[:, :], start=False, stop=True)
                if half == 1 and t % 4 in (0, 3):
                    last.then_inc(proj_done, 1)

        @block.tensor
        def _(pe):
            pe.sem_inc(scores_ready, SB)
            pe.sem_inc(probs_used, PB)
            pe.sem_inc(y_ready, YB)
            pe.wait_ge(pool_step, 3)
            pe.wait_ge(w_in, 32)
            for i in range(3):
                nc.tensor.transpose(O[:, 0, i * P:(i + 1) * P], wq_sb[:, i, :], ident[:, :])
            nc.tensor.transpose(O[:, 0, 3 * P:4 * P], wp_sb[:, :], ident[:, :]).then_inc(transposed, 1)

            def context_block(n):
                b = ORDER[n][1]
                for i in range(block_tiles(b)):
                    t = 4 * b + i
                    if t == CT:
                        pe.wait_ge(tail_in, 32)
                    elif t % STAGE == 0 or i == 0:
                        pe.wait_ge(ctx_keys_in[t // STAGE], 16)
                    src = ctx_sb[:, t, 0:C] if t < CT else tail[:, 0:C]
                    last = nc.tensor.transpose(S[:, n % 6, i * P:(i + 1) * P], src, ident[:, :])
                last.then_inc(block_ready, 1)

            for n in range(4):
                context_block(n)
            for t in range(TT):
                if t == 4:
                    pe.wait_ge(evacuated, 2)
                pe.wait_ge(xn_done, t + 1)
                last = nc.tensor.transpose(O[:, 1 - t // 4, (t % 4) * P:(t % 4 + 1) * P], xn[:, t, :], ident[:, :])
                if t % 4 == 3:
                    last.then_inc(transposed, 1)
            pe.wait_ge(evacuated, 4)
            for n in range(4, 8):
                what, i = ORDER[n]
                if n >= 6:
                    pe.wait_ge(block_read, n - 5)
                w0 = 0 if what == "q" else C
                nc.tensor.matmul(bank_of(n), wT[:, w0:w0 + C], xT[:, i * BANK:(i + 1) * BANK],
                                 start=True, stop=True).then_inc(block_ready, 1)
            for t in range(TT):
                last = nc.tensor.matmul(O[:, t // 4, (t % 4) * P:(t % 4 + 1) * P], xT[:, t * P:(t + 1) * P],
                                        wT[:, 2 * C:3 * C], start=True, stop=True)
            last.then_inc(v_self, 1)
            for n in range(8, BLOCKS):
                pe.wait_ge(block_read, n - 5)
                context_block(n)
            pe.wait_ge(kmax_done, 1)
            pe.wait_ge(qabs_done, 3)
            pe.wait_ge(v_self_out, 2)
            for half in range(2):
                nc.tensor.matmul(O[0:HEADS, half, :], blk_k[:, :], qsc[:, half * BANK:(half + 1) * BANK],
                                 start=True, stop=True).then_inc(bound_done, 1)
            pe.wait_ge(block_read, BLOCKS)
            pe.wait_ge(bound_parts, 2)
            for i in range(WARM):
                nc.tensor.matmul(S[:, 5, 0:P], ident[:, :], ident[:, :], start=True, stop=True)
            attention_pe(pe, 0)

            pe.wait_ge(flag_done, 1)
            redo = pe.value_load(lflag[0:1, 0:1], min_val=0, max_val=1)
            with pe.If(redo > 0):
                with pe.Fori(0, UNITS) as u:
                    with pe.Fori(0, NT) as t:
                        pe.wait_ge(fb_k, u * NT + t + 1)
                        for j in range(GH):
                            r = slice(64 * (j % 2), 64 * (j % 2) + SHIFT)
                            last = nc.tensor.matmul(S[:, j, :], kring[r, 0, j // 2, 0:P], qbuf[r, 0, j // 2, :],
                                                    start=True, stop=True)
                        last.then_inc(fb_s, 1)
                pe.wait_ge(linv_done, LB + UNITS)
                attention_pe(pe, 1)
                pe.wait_ge(normed, 2 * UNITS)

            pe.wait_ge(normed, UNITS)
            project(1)
            for t in range(TT):
                pe.wait_ge(x2n_done, t + 1)
                last = nc.tensor.transpose(S[:, t // 4, (t % 4) * P:(t % 4 + 1) * P], xn[:, t, :], ident[:, :])
                if t % 4 == 3:
                    last.then_inc(transposed2, 1)
            pe.wait_ge(evacuated2, 2)
            for t in range(TT):
                last = nc.tensor.matmul(S[:, 5, t * EXPERTS:(t + 1) * EXPERTS], xT[:, t * P:(t + 1) * P], gw_sb[:, :],
                                        start=True, stop=True)
            last.then_inc(logits_ready, 1)

            down_banks = [O[:, 0, 0:C], O[:, 1, 0:C], S[:, 4, 0:C], S[:, 5, 0:C]]

            def two_experts(pair, first=False):
                for k in range(2):
                    e = pair * 2 + k
                    pe.wait_ge(expert_in[k], pair * 48 + 48)
                    for half in range(2):
                        for f in range(FFC):
                            pe.wait_ge(gelu_done, e * 8 + (4 * half + f - 3 + GB))
                            nc.tensor.matmul(S[:, f, :], w1_sb[:, k, f * P:(f + 1) * P],
                                             xT[:, half * BANK:(half + 1) * BANK], start=True, stop=True).then_inc(hidden_ready, 1)
                    if first and k == 0:
                        pe.wait_ge(shifted_logits, 1)
                    if not first and k == 0:
                        pe.wait_ge(b2_added, 2)
                    for half in range(2):
                        pe.wait_ge(gelu_done, e * 8 + (4 * half + 4 + GB))
                        if first and k == 1 and half == 1:
                            pe.wait_ge(rw_done, 1)
                            for t in range(TT):
                                last = nc.tensor.transpose(S[0:EXPERTS, t // 4, (t % 4) * P:(t % 4 + 1) * P], rw[:, t, :], ident[:, :])
                            last.then_inc(rwT_ready, 1)
                        for i in range(4):
                            pe.wait_ge(y_added, e * 8 + (4 * half + i - 3 + YB))
                            for f in range(FFC):
                                last = nc.tensor.matmul(down_banks[i], hT[:, half, f, i * P:(i + 1) * P], w2_sb[:, k, f, :],
                                                        start=(f == 0), stop=(f == FFC - 1))
                            last.then_inc(y_ready, 1)

            two_experts(0, first=True)
            pe.wait_ge(rwT_copied, 1)
            pe.wait_ge(y_added, YB + 2 * TT - 2)
            for t in range(TT):
                last = nc.tensor.matmul(O[:, t // 4, (t % 4) * P:(t % 4 + 1) * P], rwT[:, t * P:(t + 1) * P], b2_sb[:, :],
                                        start=True, stop=True)
            last.then_inc(b2_ready, 1)
            with pe.Fori(1, EXPERTS // 2) as pair:
                two_experts(pair)

        def attention_act(act, base):
            def exps(half, e, u, step=0, first_step=False):
                first, end = TAKE * e, min(TAKE * (e + 1), BANKS)
                if first_step and end <= P_BANKS:
                    tile = min((end + BANKS - P_BANKS) // GH, NT - 1) - NT
                else:
                    tile = (end - 1 - P_BANKS) // GH
                act.wait_ge(probs_used, u * NT + (tile + 1 + PB) + step * STEP)
                act.wait_ge(scores_ready, u * EXPS + (e + 1 + SB) + step * 2 * CHUNK_EXPS)
                p0 = (first + half * (P_BANKS // 2)) % P_BANKS
                nc.scalar.activation(probs[:, p0:p0 + end - first, :], S[:, first % S_BANKS:first % S_BANKS + end - first, :],
                                     ACT.Exp).then_inc(exp_done, 1)

            with act.Fori(0, GROUPS) as g:
                for half in range(2):
                    u = g * 2 + (UNITS * base + half)
                    for e in range(2 * CHUNK_EXPS):
                        exps(half, e, u, first_step=True)
                    with act.Fori(1, STEPS) as i:
                        for e in range(2 * CHUNK_EXPS):
                            exps(half, e, u, i)
                    for e in range(STEPS * 2 * CHUNK_EXPS, EXPS):
                        exps(half, e, u)

        @block.scalar
        def _(act):
            act.sem_inc(exp_done, EB)
            act.sem_inc(gelu_done, GB)
            act.wait_ge(transposed, 1)
            nc.scalar.activation(wT[:, :], O[:, 0, 0:3 * C], ACT.Copy).then_inc(evacuated, 1)
            nc.scalar.activation(wpT_sb[:, :], O[:, 0, 3 * C:4 * C], ACT.Copy).then_inc(evacuated, 1)
            act.wait_ge(evacuated, 2)
            act.sem_inc(wpt_ready, 1)
            act.wait_ge(ln_stats, 1)
            nc.scalar.activation(std[:, :], mv[:, :, 1], ACT.Sqrt).then_inc(std_done, 1)

            def part1(n):
                act.wait_ge(block_ready, n + 1)
                if n >= 4:
                    act.wait_ge(parts_out[n % 4], outs(n))
                src = bank_of(n)
                what, i = ORDER[n]
                if what == "q":
                    q = qsc[:, i * BANK:(i + 1) * BANK]
                    nc.scalar.activation(q, src, ACT.Copy, scale=SCALE).then_inc(qabs_done, 1)
                    act.wait_ge(qabs_done, i + 1)
                    src = q
                nc.scalar.activation(part_slots[n % 4][:, 0, 0:width(n)], src, ACT.Copy).then_inc(part1_done, 1)

            part1(0)
            for n in range(BLOCKS):
                if n == 3:
                    for half in range(2):
                        act.wait_ge(transposed, 2 + half)
                        nc.scalar.activation(xT[:, half * BANK:(half + 1) * BANK], O[:, 1 - half, :], ACT.Copy).then_inc(evacuated, 1)
                if n + 1 < BLOCKS:
                    part1(n + 1)
                act.wait_ge(rest_done, n + 1)
                nc.scalar.activation(part_slots[n % 4][:, 1, 0:width(n)], rest[:, n % 2, 0:width(n)], ACT.Copy).then_inc(part2_done, 1)
                if n in VALUES_AT:
                    i = VALUES_AT.index(n)
                    act.wait_ge(ctx_values_in[i], 16)
                    act.wait_ge(pool_step, 9)
                    src = ctx_sb[:, i * STAGE:(i + 1) * STAGE, C:2 * C].rearrange("p t (h d) -> p t h d", d=D)
                    nc.scalar.activation(vres[:, TT + i * STAGE:TT + (i + 1) * STAGE, :, 0:D], src, ACT.Copy).then_inc(values_done, 1)
                if ORDER[n] == ("q", 1):
                    nc.scalar.activation(qsc[:, :], qsc[:, :], ACT.Abs).then_inc(qabs_done, 1)
            act.wait_ge(small_in, SMALL)
            nc.scalar.activation(tg[:, :], gates[:, :], ACT.Tanh).then_inc(act_step, 1)
            act.wait_ge(values_done, CT // STAGE)
            act.wait_ge(block_read, BLOCKS)
            attention_act(act, 0)
            act.wait_ge(flag_done, 1)
            redo = act.value_load(lflag[0:1, 0:1], min_val=0, max_val=1)
            with act.If(redo > 0):
                act.wait_ge(fb_rows_in, 16 * 6 * UNITS)
                attention_act(act, 1)
                act.wait_ge(normed, 2 * UNITS)
            act.wait_ge(x1_stats, 1)
            nc.scalar.activation(std[:, :], mv[:, :, 1], ACT.Sqrt).then_inc(std2_done, 1)
            for half in range(2):
                act.wait_ge(transposed2, 1 + half)
                nc.scalar.activation(xT[:, half * BANK:(half + 1) * BANK], S[:, half, :], ACT.Copy).then_inc(evacuated2, 1)

            def load_gelu(i):
                nc.scalar.activation(unread[:, i:i + 1], tg[:, 0:1], ACT.Gelu).then_inc(act_step, 1)

            def two_experts(pair, first=False):
                for k in range(2):
                    e = pair * 2 + k
                    act.wait_ge(expert_in[k], pair * 48 + 48)
                    for half in range(2):
                        if not (first and k == 0):
                            act.wait_ge(y_ready, e * 8 + (4 * half - 4 + YB))
                        for f in range(FFC):
                            act.wait_ge(hidden_ready, e * 8 + (4 * half + f + 1))
                            nc.scalar.activation(hT[:, half, f, :], S[:, f, :], ACT.Gelu,
                                                 bias=b1_now[:, k, f:f + 1]).then_inc(gelu_done, 1)
                        if first and k == 0 and half == 1:
                            act.wait_ge(shifted_logits, 1)
                            nc.scalar.activation(le[:, :, :], lt[:, :, :], ACT.Exp).then_inc(router_exp, 1)
                            load_gelu(1)

            load_gelu(0)
            two_experts(0, first=True)
            with act.Fori(1, EXPERTS // 2) as pair:
                two_experts(pair)

        def norm_stats(dve, t0, t1, before=0):
            for t in range(t0, t1):
                nc.vector.bn_stats(stats[:, t, :], xs[:, t, :]).then_inc(bn_done, 1)
            dve.wait_ge(bn_done, before + t1)
            for t in range(t0, t1):
                nc.vector.bn_aggr(mv[:, t, :], stats[:, t, :]).then_inc(aggregated, 1)

        def layer_norm(dve, link, count, stats_done, std_ready, out_done):
            dve.wait_ge(aggregated, count)
            nc.vector.tensor_scalar(mv[:, :, 1], mv[:, :, 1], EPS, None, ALU.add).then_inc(stats_done, 1)
            dve.wait_ge(std_ready, 1)
            link(nc.vector.reciprocal(rstd[:, :], std[:, :]))
            for t in range(TT):
                nc.vector.tensor_scalar(xn[:, t, :], xs[:, t, :], mv[:, t, 0:1], rstd[:, t:t + 1],
                                        ALU.subtract, ALU.mult).then_inc(out_done, 1)

        def copy(dst, src):
            return nc.vector.tensor_scalar(dst, src, 1.0, None, ALU.mult)

        def attention_dve(dve, base):
            def chunk(c, unit, step=0, start=False):
                u, pair0, g = UNITS * base + unit, 2 * (unit // 2 % 2), unit // 2
                full = min(CHUNK, NT - 1 - CHUNK * c)
                w = full * P + (32 if c == CHUNKS - 1 else 0)
                tiles = CHUNK * (CHUNKS - 1) - NT if start and c == 0 else CHUNK * (c - 1)
                if u or not start:
                    exps = -(EXPS - CHUNK_EXPS * (CHUNKS - 1)) if start and c == 0 else CHUNK_EXPS * (c - 1)
                    dve.wait_ge(scores_ready, u * EXPS + (exps + SB) + step * 2 * CHUNK_EXPS)
                copy(kring[:, c % 2, :, 0:w],
                     kst[:, pair0:pair0 + 2, bass.ds(step * (STEP * P) + c * CHUNK * P, w)]).then_inc(k_ready, 1)
                if u or not start:
                    dve.wait_ge(probs_used, u * NT + (tiles + PB) + step * STEP)
                if c == CHUNKS - 1:
                    dve.wait_ge(last_values_in, 16 * GH)
                    copy(vlast_now[:, :], vlast[:, g, :])
                copy(vring[:, c % 2, 0:full, :, 0:D + 1],
                     vres[:, bass.ds(step * STEP + c * CHUNK, full), g * GH:(g + 1) * GH, :]).then_inc(v_ready, 1)

            def copy_out(unit):
                if unit < 2:
                    dve.wait_ge(uraw_set, 1)
                dve.wait_ge(probs_used, (UNITS * base + unit + 1) * NT + PB)
                if unit >= 2:
                    dve.wait_ge(normed, UNITS * base + unit - 1)
                nc.vector.tensor_copy(Uraw[:, unit % 2, :], O[:, unit % 2, :]).then_inc(o_copied, 1)

            def invert(unit):
                dve.wait_ge(l_ready, (UNITS + 1) * base + unit + 2)
                nc.vector.tensor_reduce(lmin[:, unit:unit + 1], O[:, unit % 2, :], axis=AX.X, op=ALU.min)
                nc.vector.reciprocal(linv[:, unit % 2, :], O[:, unit % 2, :]).then_inc(linv_done, 1)

            def normalise(unit):
                dve.wait_ge(linv_done, LB + UNITS * base + unit + 1)
                nc.vector.tensor_tensor(U[:, unit // 2, (unit % 2) * HALF:(unit % 2 + 1) * HALF],
                                        Uraw[:, unit % 2, :], linv[:, unit % 2, :], ALU.mult).then_inc(normed, 1)

            for unit in range(UNITS):
                g, half = unit // 2, unit % 2
                first = unit == 0 and base == 0
                if half == 0:
                    dve.wait_ge(k_stack_in, 16 * K_LOADS if first else stacks_in(2 * GROUPS * base + g))
                nc.vector.tensor_copy(qbuf[:, half, :, :],
                                      qst[:, 2 * g:2 * g + 2, half * HALF:(half + 1) * HALF]).then_inc(q_ready, 1)
                chunk(0, unit, start=True)
                chunk(1, unit, start=True)
                if unit:
                    copy_out(unit - 1)
                if first:
                    dve.wait_ge(k_stack_in, stacks_in(0))
                with dve.Fori(1, STEPS) as i:
                    chunk(0, unit, i)
                    chunk(1, unit, i)
                chunk(CHUNKS - 2, unit)
                if unit:
                    invert(unit - 1)
                chunk(CHUNKS - 1, unit)
                if unit:
                    normalise(unit - 1)
            copy_out(UNITS - 1)
            invert(UNITS - 1)
            normalise(UNITS - 1)

        @block.vector
        def _(dve):
            steps = [0]

            def link(ins):
                steps[0] += 1
                ins.then_inc(dve_step, 1)
                dve.wait_ge(dve_step, steps[0])

            dve.wait_ge(x_in, 16)
            norm_stats(dve, 0, TT)
            layer_norm(dve, link, TT, ln_stats, std_done, xn_done)

            dve.wait_ge(pool_step, 3)
            link(nc.vector.tensor_reduce(blk[:, :], ident[:, :].rearrange("p (h d) -> p h d", d=D), axis=AX.X, op=ALU.add))

            column = 0
            for n in range(BLOCKS):
                what, i = ORDER[n]
                w = width(n)
                dve.wait_ge(part1_done, n + 1)
                if n >= 2:
                    dve.wait_ge(part3_done, n - 1)
                src = qsc[:, i * BANK:(i + 1) * BANK] if what == "q" else bank_of(n)
                nc.vector.tensor_tensor(rest[:, n % 2, 0:w], src, part_slots[n % 4][:, 0, 0:w], ALU.subtract).then_inc(rest_done, 1)
                if what == "q":
                    dve.wait_ge(rest_done, n + 1)
                    dve.sem_inc(block_read, 1)
                else:
                    nc.vector.tensor_reduce(kabs[:, column:column + 1], src, axis=AX.X, op=ALU.max,
                                            apply_absolute_value=True).then_inc(block_read, 1)
                    column += 1
                if n == 9:
                    dve.wait_ge(v_self, 1)
                    for half in range(2):
                        nc.vector.tensor_copy(vres[:, 4 * half:4 * half + 4, :, 0:D],
                                              O[:, half, :].rearrange("p (t h d) -> p t h d", h=HEADS, d=D)).then_inc(v_self_out, 1)
            dve.wait_ge(block_read, BLOCKS)
            link(nc.vector.tensor_reduce(kmax[:, :], kabs[:, 0:column], axis=AX.X, op=ALU.max))
            nc.vector.tensor_scalar(blk_k[:, :], blk[:, :], kmax[:, 0:1], None, ALU.mult).then_inc(kmax_done, 1)
            dve.wait_ge(part3_done, BLOCKS)
            dve.wait_ge(values_done, CT // STAGE)
            for half in range(2):
                dve.wait_ge(bound_done, half + 1)
                m3 = mparts[:, :, half * HALF:(half + 1) * HALF]
                link(nc.vector.tensor_scalar(mneg[:, half, :], O[0:HEADS, half, :], -BOUND_SLACK, -BOUND_MAX, ALU.mult, ALU.max))
                link(nc.vector.tensor_copy(m3[:, 0, :], mneg[:, half, :]))
                link(nc.vector.tensor_tensor(mrem[:, half, :], mneg[:, half, :], m3[:, 0, :], ALU.subtract))
                link(nc.vector.tensor_copy(m3[:, 1, :], mrem[:, half, :]))
                nc.vector.tensor_tensor(m3[:, 2, :], mrem[:, half, :], m3[:, 1, :], ALU.subtract).then_inc(bound_parts, 1)

            dve.sem_inc(o_copied, OB)
            dve.sem_inc(linv_done, LB)
            dve.sem_inc(y_added, YB)
            for slot in range(2, 4):
                dve.wait_ge(parts_out[slot], outs(BLOCKS - 1 - (BLOCKS - 1 - slot) % 4 + 4))
            dve.wait_ge(pool_step, 9)
            dve.wait_ge(v_self_out, 2)
            nc.vector.memset(Uraw[:, :, :], 1.0).then_inc(uraw_set, 1)
            dve.wait_ge(q_stack_in, 16 * (2 * SLOTS + 2))
            attention_dve(dve, 0)
            dve.wait_ge(normed, UNITS)
            link(nc.vector.tensor_reduce(kmax[:, :], lmin[:, :], axis=AX.X, op=ALU.min))
            nc.vector.tensor_scalar(lneg[:, :], kmax[:, :], -1.0, None, ALU.mult).then_inc(lneg_done, 1)
            dve.wait_ge(lall_done, 1)
            nc.vector.tensor_scalar(lflag[:, :], lall[:, :], -L_MIN, None, ALU.is_gt).then_inc(flag_done, 1)
            dve.wait_ge(flag_done, 1)
            redo = dve.value_load(lflag[0:1, 0:1], min_val=0, max_val=1)
            with dve.If(redo > 0):
                with dve.Fori(0, GROUPS // 2) as gg:
                    for parity in range(2):
                        g = gg * 2 + parity
                        dve.wait_ge(k_stack_in, gg * (2 * 16 * K_LOADS) + stacks_in(GROUPS + parity))
                        for half in range(2):
                            u = gg * 4 + (2 * parity + half)
                            copy(qbuf[:, 0, :, :], qst[:, bass.ds(g * 2, 2), half * HALF:(half + 1) * HALF]).then_inc(fb_m, 1)
                            nc.vector.memset(runmax, -3.0e38).then_inc(fb_m, 1)
                            with dve.Fori(0, NT) as t:
                                copy(kring[:, 0, :, 0:P],
                                                      kst[:, 2 * parity:2 * parity + 2, bass.ds(t * P, P)]).then_inc(fb_k, 1)
                                dve.wait_ge(fb_s, u * NT + t + 1)
                                dve.wait_ge(fb_m, u * (NT + 2) + t + 2)
                                nc.vector.tensor_tensor(runmax, runmax, S[:, 0:4, :], ALU.max).then_inc(fb_m, 1)
                                dve.wait_ge(fb_m, u * (NT + 2) + t + 3)
                            nc.vector.memset(mrest, 0.0).then_inc(fb_max, 1)
                            dve.wait_ge(fb_all, u + 1)
                            dve.wait_ge(fb_rows_in, u * 96)
                            nc.vector.tensor_scalar(mrow, allmax[0:1, :], -1.0, None, ALU.mult).then_inc(fb_neg, 1)
                            dve.wait_ge(fb_neg, u * 4 + 1)
                            nc.vector.tensor_copy(rowparts[:, 0, :], mrow).then_inc(fb_neg, 1)
                            dve.wait_ge(fb_neg, u * 4 + 2)
                            nc.vector.tensor_tensor(mrest, mrow, rowparts[:, 0, :], ALU.subtract).then_inc(fb_neg, 1)
                            dve.wait_ge(fb_neg, u * 4 + 3)
                            nc.vector.tensor_copy(rowparts[:, 1, :], mrest).then_inc(fb_neg, 1)
                            dve.wait_ge(fb_neg, u * 4 + 4)
                            nc.vector.tensor_tensor(rowparts[:, 2, :], mrest, rowparts[:, 1, :], ALU.subtract).then_inc(fb_rows, 1)
                            dve.wait_ge(fb_rows, u + 1)
                            dve.sem_inc(fb_units, 1)
                dve.wait_ge(fb_rows_in, 96 * UNITS)
                attention_dve(dve, 1)
                dve.wait_ge(normed, 2 * UNITS)

            dve.wait_ge(act_step, 1)
            for half in range(2):
                dve.wait_ge(proj_done, half + 1)
                rows = xs[:, 4 * half:4 * half + 4, :]
                nc.vector.scalar_tensor_tensor(out=rows, in0=O[:, half, :].rearrange("p (t c) -> p t c", t=4), scalar=tg[:, 0:1],
                                               in1=rows, op0=ALU.mult, op1=ALU.add).then_inc(x1_done, 1)
                dve.wait_ge(x1_done, half + 1)
                norm_stats(dve, 4 * half, 4 * half + 4, TT)

            steps2 = [0]

            def second(ins):
                steps2[0] += 1
                ins.then_inc(tail_step, 1)
                dve.wait_ge(tail_step, steps2[0])

            layer_norm(dve, second, 2 * TT, x1_stats, std2_done, x2n_done)
            dve.wait_ge(logits_ready, 1)
            second(nc.vector.tensor_copy(lg[:, :, :], S[:, 5, 0:TT * EXPERTS].rearrange("p (t e) -> p t e", t=TT)))
            second(nc.vector.tensor_reduce(r1[:, 0, :], lg[:, :, :], axis=AX.X, op=ALU.max))

            def spread(i):
                return r1[:, i, :].rearrange("p (t o) -> p t o", o=1).broadcast_to([P, TT, EXPERTS])

            nc.vector.tensor_tensor(lt[:, :, :], lg[:, :, :], spread(0), ALU.subtract).then_inc(shifted_logits, 1)
            dve.wait_ge(shifted_logits, 1)
            second(nc.vector.tensor_scalar(cand[:, :, :], lt[:, :, :], 0.0, float(EXPERTS), ALU.is_lt, ALU.mult))
            second(nc.vector.tensor_tensor(cand[:, :, :], cand[:, :, :], iota8[:, :, :], ALU.add))
            second(nc.vector.tensor_reduce(r1[:, 1, :], cand[:, :, :], axis=AX.X, op=ALU.min))
            second(nc.vector.tensor_tensor(cand[:, :, :], cand[:, :, :], spread(1), ALU.is_equal))
            dve.wait_ge(router_exp, 1)
            second(nc.vector.tensor_reduce(r1[:, 2, :], le[:, :, :], axis=AX.X, op=ALU.add))
            second(nc.vector.reciprocal(r1[:, 3, :], r1[:, 2, :]))
            second(nc.vector.tensor_tensor(cand[:, :, :], cand[:, :, :], spread(3), ALU.mult))
            nc.vector.tensor_scalar(rw[:, :, :], cand[:, :, :], tg[:, 1:2], None, ALU.mult).then_inc(rw_done, 1)
            dve.wait_ge(rw_done, 1)
            down_banks = [O[:, 0, 0:C], O[:, 1, 0:C], S[:, 4, 0:C], S[:, 5, 0:C]]

            def add_expert(e, tiles):
                for t in tiles:
                    dve.wait_ge(y_ready, e * 8 + (t + 1 + YB))
                    dve.wait_ge(y_added, e * 8 + (t - 7 + YB))
                    nc.vector.scalar_tensor_tensor(out=xs[:, t, :], in0=down_banks[t % 4], scalar=rw[:, t, bass.ds(e, 1)],
                                                   in1=xs[:, t, :], op0=ALU.mult, op1=ALU.add).then_inc(y_added, 1)

            add_expert(0, range(TT))
            add_expert(1, range(TT // 2))
            dve.wait_ge(rwT_ready, 1)
            nc.vector.tensor_copy(rwT.rearrange("e (s q) -> e s q", s=2), S[0:EXPERTS, 0:2, :]).then_inc(rwT_copied, 1)
            add_expert(1, range(TT // 2, TT))
            dve.wait_ge(b2_ready, 1)
            dve.wait_ge(y_added, YB + 2 * TT)
            for half in range(2):
                rows = xs[:, 4 * half:4 * half + 4, :]
                nc.vector.tensor_tensor(rows, O[:, half, :].rearrange("p (t c) -> p t c", t=4), rows, ALU.add).then_inc(b2_added, 1)
            dve.wait_ge(b2_added, 2)
            with dve.Fori(2, EXPERTS) as e:
                add_expert(e, range(TT))


_INS = ['x', 'ctx_2048', 'g_xattn', 'g_ffn', 'L0_xattn_w_qkv', 'L0_xattn_w_proj', 'L0_xattn_b_proj',
        'L0_ffn_gate_w', 'L0_ffn_w1', 'L0_ffn_b1', 'L0_ffn_w2', 'L0_ffn_b2']


def kernel(**inputs):
    import numpy as _np
    import concourse.bacc as _bacc
    from concourse import mybir as _mybir
    from concourse.bass_utils import run_bass_kernel_spmd as _run

    nc = _bacc.Bacc("TRN2", target_bir_lowering=False, num_devices=1)
    arrays, args = {}, []
    for name in _INS:
        a = _np.ascontiguousarray(inputs[name])
        arrays[f"in_{name}_dram"] = a
        args.append(nc.dram_tensor(f"in_{name}_dram", a.shape, _mybir.dt.from_np(a.dtype), kind="ExternalInput").ap())
    args.append(nc.dram_tensor("out_0_dram", (1, TOKENS, C), _mybir.dt.float32, kind="ExternalOutput").ap())
    for name, shape, dt in (("k_parts", (3, HEADS, D, KEYS), BF16), ("q_parts", (3, HEADS, D, TOKENS), BF16),
                            ("bound_rows", (3, HEADS, TOKENS), BF16), ("proj_t", (P, C), F32)):
        args.append(nc.dram_tensor(name, shape, dt).ap())
    program(nc, *args)
    r = _run(nc, [arrays], core_ids=[0])
    return r.results[0]["out_0_dram"]
```
